# Optimizing a Trainium2 kernel written in Bass

```python
import numpy as np
import jax
import jax.numpy as jnp

def _softmax(x, axis=-1):
    return jax.nn.softmax(x, axis=axis)

def _gelu(x):
    return jax.nn.gelu(x, approximate=True)

def _silu(x):
    return jax.nn.silu(x)

def _sigmoid(x):
    return jax.nn.sigmoid(x)

def _layernorm(x, axis=-1, eps=1e-05):
    m = jnp.mean(x, axis=axis, keepdims=True)
    v = jnp.var(x, axis=axis, keepdims=True)
    return (x - m) / jnp.sqrt(v + eps)

def _scatter_add(tgt, idx, src, axis=0):
    return tgt.at[idx].add(src)

def _segment_sum(src, seg, n):
    return jax.ops.segment_sum(src, seg, n)
kernel_name = 'mk_sandwich_d1_jaxref_r4_64e541'

def setup_inputs(seed: int=0):
    np.random.seed(seed)
    _w = jnp.asarray

    def _L0_attn_setup():
        import math
        import jax, jax.numpy as jnp
        import numpy as np
        D_MODEL = 256
        N_HEADS = 16
        HEAD_DIM = D_MODEL // N_HEADS
        ROPE_BASE = 10000.0
        EPS = 1e-06

        def rmsnorm(x, w, eps=EPS):
            xf = x.astype(jnp.float32)
            rms = jax.lax.rsqrt(jnp.mean(xf * xf, axis=-1, keepdims=True) + eps)
            return (xf * rms).astype(x.dtype) * w

        def apply_rope(x, cos, sin):
            d2 = x.shape[-1] // 2
            x1, x2 = (x[..., :d2], x[..., d2:])
            c = cos[None, None, :, :]
            s = sin[None, None, :, :]
            return jnp.concatenate([x1 * c - x2 * s, x2 * c + x1 * s], axis=-1)
        key = jax.random.key(seed)
        ks = jax.random.split(key, 7)
        B, T = (2, 512)
        x = jax.random.normal(ks[0], (B, T, D_MODEL), dtype=jnp.float32)
        scale = 1.0 / math.sqrt(D_MODEL)
        Wq = jax.random.normal(ks[1], (D_MODEL, D_MODEL), dtype=jnp.float32) * scale
        Wk = jax.random.normal(ks[2], (D_MODEL, D_MODEL), dtype=jnp.float32) * scale
        Wv = jax.random.normal(ks[3], (D_MODEL, D_MODEL), dtype=jnp.float32) * scale
        Wo = jax.random.normal(ks[4], (D_MODEL, D_MODEL), dtype=jnp.float32) * scale
        q_norm_w = jnp.ones((HEAD_DIM,), dtype=jnp.float32)
        k_norm_w = jnp.ones((HEAD_DIM,), dtype=jnp.float32)
        return {'x': x, 'Wq': Wq, 'Wk': Wk, 'Wv': Wv, 'Wo': Wo, 'q_norm_w': q_norm_w, 'k_norm_w': k_norm_w}
    _L0_attn_in = _L0_attn_setup()

    def _L0_ffn_setup():
        import jax, jax.numpy as jnp
        import numpy as np
        D_IN, D_HID = (256, 1024)

        def _ternary(key, shape):
            return jax.random.randint(key, shape, -1, 2).astype(jnp.float32)

        def _tlin(x, w, s):
            return jnp.einsum('bsi,oi->bso', x, w) * s
        key = jax.random.key(seed)
        ks = jax.random.split(key, 12)
        inv = lambda fan: 1.0 / np.sqrt(fan).astype(np.float32)
        return {'x': jax.random.normal(ks[0], (4, 512, D_IN), dtype=jnp.float32), 'w1_w': _ternary(ks[1], (D_HID, D_IN)), 'w1_s': jax.random.uniform(ks[2], (D_HID,), dtype=jnp.float32) * inv(D_IN), 'w2_w': _ternary(ks[3], (D_HID, D_IN)), 'w2_s': jax.random.uniform(ks[4], (D_HID,), dtype=jnp.float32) * inv(D_IN), 'h1_w': _ternary(ks[5], (D_HID, D_HID)), 'h1_s': jax.random.uniform(ks[6], (D_HID,), dtype=jnp.float32) * inv(D_HID), 'h2_w': _ternary(ks[7], (D_HID, D_HID)), 'h2_s': jax.random.uniform(ks[8], (D_HID,), dtype=jnp.float32) * inv(D_HID), 'w3_w': _ternary(ks[9], (D_IN, D_HID)), 'w3_s': jax.random.uniform(ks[10], (D_IN,), dtype=jnp.float32) * inv(D_HID)}
    _L0_ffn_in = _L0_ffn_setup()
    _d = {'L0_attn_x': _L0_attn_in['x'], 'L0_attn_Wq': _L0_attn_in['Wq'], 'L0_attn_Wk': _L0_attn_in['Wk'], 'L0_attn_Wv': _L0_attn_in['Wv'], 'L0_attn_Wo': _L0_attn_in['Wo'], 'L0_attn_q_norm_w': _L0_attn_in['q_norm_w'], 'L0_attn_k_norm_w': _L0_attn_in['k_norm_w'], 'L0_ffn_w1_w': _L0_ffn_in['w1_w'], 'L0_ffn_w1_s': _L0_ffn_in['w1_s'], 'L0_ffn_w2_w': _L0_ffn_in['w2_w'], 'L0_ffn_w2_s': _L0_ffn_in['w2_s'], 'L0_ffn_h1_w': _L0_ffn_in['h1_w'], 'L0_ffn_h1_s': _L0_ffn_in['h1_s'], 'L0_ffn_h2_w': _L0_ffn_in['h2_w'], 'L0_ffn_h2_s': _L0_ffn_in['h2_s'], 'L0_ffn_w3_w': _L0_ffn_in['w3_w'], 'L0_ffn_w3_s': _L0_ffn_in['w3_s']}
    _x0 = _d['L0_attn_x']
    _d['L0_attn_x'] = jax.random.normal(jax.random.fold_in(jax.random.key(seed), 1), (2, 2048, 256), dtype=_x0.dtype)
    del _x0
    return _d

def reference(L0_attn_x, L0_attn_Wq, L0_attn_Wk, L0_attn_Wv, L0_attn_Wo, L0_attn_q_norm_w, L0_attn_k_norm_w, L0_ffn_w1_w, L0_ffn_w1_s, L0_ffn_w2_w, L0_ffn_w2_s, L0_ffn_h1_w, L0_ffn_h1_s, L0_ffn_h2_w, L0_ffn_h2_s, L0_ffn_w3_w, L0_ffn_w3_s):

    def _L0_attn_ref(x, Wq, Wk, Wv, Wo, q_norm_w, k_norm_w):
        import math
        import jax, jax.numpy as jnp
        import numpy as np
        D_MODEL = 256
        N_HEADS = 16
        HEAD_DIM = D_MODEL // N_HEADS
        ROPE_BASE = 10000.0
        EPS = 1e-06

        def rmsnorm(x, w, eps=EPS):
            xf = x.astype(jnp.float32)
            rms = jax.lax.rsqrt(jnp.mean(xf * xf, axis=-1, keepdims=True) + eps)
            return (xf * rms).astype(x.dtype) * w

        def apply_rope(x, cos, sin):
            d2 = x.shape[-1] // 2
            x1, x2 = (x[..., :d2], x[..., d2:])
            c = cos[None, None, :, :]
            s = sin[None, None, :, :]
            return jnp.concatenate([x1 * c - x2 * s, x2 * c + x1 * s], axis=-1)
        B, T, d = x.shape
        H, hd = (N_HEADS, HEAD_DIM)
        q = (x @ Wq).reshape(B, T, H, hd).transpose(0, 2, 1, 3)
        k = (x @ Wk).reshape(B, T, H, hd).transpose(0, 2, 1, 3)
        v = (x @ Wv).reshape(B, T, H, hd).transpose(0, 2, 1, 3)
        q = rmsnorm(q, q_norm_w)
        k = rmsnorm(k, k_norm_w)
        inv_freq = 1.0 / ROPE_BASE ** (jnp.arange(0, hd, 2, dtype=jnp.float32) / hd)
        t = jnp.arange(T, dtype=jnp.float32)
        freqs = jnp.outer(t, inv_freq)
        cos, sin = (jnp.cos(freqs), jnp.sin(freqs))
        q = apply_rope(q, cos, sin)
        k = apply_rope(k, cos, sin)
        scale = 1.0 / math.sqrt(hd)
        attn = jnp.einsum('bhqd,bhkd->bhqk', q, k) * scale
        causal = jnp.triu(jnp.full((T, T), -jnp.inf, dtype=attn.dtype), k=1)
        attn = attn + causal[None, None, :, :]
        attn = jax.nn.softmax(attn, axis=-1)
        out = jnp.einsum('bhqk,bhkd->bhqd', attn, v)
        out = out.transpose(0, 2, 1, 3).reshape(B, T, d)
        return out @ Wo

    def _L0_ffn_ref(x, w1_w, w1_s, w2_w, w2_s, h1_w, h1_s, h2_w, h2_s, w3_w, w3_s):
        import jax, jax.numpy as jnp
        import numpy as np
        D_IN, D_HID = (256, 1024)

        def _ternary(key, shape):
            return jax.random.randint(key, shape, -1, 2).astype(jnp.float32)

        def _tlin(x, w, s):
            return jnp.einsum('bsi,oi->bso', x, w) * s
        h = jax.nn.silu(_tlin(x, w1_w, w1_s)) * _tlin(x, w2_w, w2_s)
        h = jax.nn.gelu(_tlin(h, h1_w, h1_s), approximate=False)
        h = jax.nn.gelu(_tlin(h, h2_w, h2_s), approximate=False)
        return _tlin(h, w3_w, w3_s)
    x = L0_attn_x
    x = x + _layernorm(_L0_attn_ref(_layernorm(x, axis=-1), L0_attn_Wq, L0_attn_Wk, L0_attn_Wv, L0_attn_Wo, L0_attn_q_norm_w, L0_attn_k_norm_w), axis=-1)
    x = x + _layernorm(_L0_ffn_ref(_layernorm(x, axis=-1), L0_ffn_w1_w, L0_ffn_w1_s, L0_ffn_w2_w, L0_ffn_w2_s, L0_ffn_h1_w, L0_ffn_h1_s, L0_ffn_h2_w, L0_ffn_h2_s, L0_ffn_w3_w, L0_ffn_w3_s), axis=-1)
    return x

_drawn_inputs = setup_inputs


def setup_inputs(seed=0):
    import zlib

    import numpy as np

    out = dict(_drawn_inputs(seed))
    spreads = {'L0_attn_q_norm_w': (1.0, 0.2), 'L0_attn_k_norm_w': (1.0, 0.2)}
    factors = {}
    for name, (base, spread) in spreads.items():
        noise = np.random.default_rng([zlib.crc32(name.encode()), seed]).standard_normal(out[name].shape)
        drawn = base * np.exp(spread * noise) if base else spread * noise
        out[name] = jnp.asarray(drawn.astype(out[name].dtype))
    for name, factor in factors.items():
        out[name] = (out[name] * factor).astype(out[name].dtype)
    return out
```

```python
from contextlib import ExitStack

import numpy as np
import concourse.bass as bass
from concourse import mybir

F32 = mybir.dt.float32
F32R = mybir.dt.float32r
ALU = mybir.AluOpType
ACT = mybir.ActivationFunctionType
AX = mybir.AxisListType

P = 128
B, T, D = 2, 2048, 256
H, HD = 16, 16
HID = 1024
NT = B * T // P
TPB = T // P
DC = D // P
HC = HID // P
QH = 4
NU = B * H // QH
QW = 512
NQT = T // QW
KPQ = QW // P
ROWS = 4 * HD + 1
STRIP = 32
LN_EPS = 1e-5
RMS_EPS = 1e-6
MASKED = -1e30
TG = 4
NG = NT // TG


def at(it, per, n):
    return it * per + n


def wait(eng, sem, value):
    if not isinstance(value, int) or value > 0:
        eng.wait_ge(sem, value)


def wait_apart(eng, passed, sem, value):
    eng.wait_ge(sem, value)
    eng.sem_inc(passed, 1)


class Chain:

    def __init__(self, eng, passed, sem, base=0):
        self.eng, self.passed, self.sem, self.base, self.n = eng, passed, sem, base, 0

    def __call__(self, ins):
        self.n += 1
        ins.then_inc(self.sem, 1)
        wait_apart(self.eng, self.passed, self.sem, self.base + self.n)


def peeled(eng, n, body):
    body(0, True, False)
    with eng.Fori(1, n - 1) as it:
        body(it, False, False)
    body(n - 1, False, True)


def score_banks():
    out = []
    for qt in reversed(range(NQT)):
        banks, k0 = [], KPQ * qt
        for h in range(QH):
            banks.append(([(k0, h, 0, 512, 0)], [0]))
        for h in range(QH):
            banks.append(([(k0 + 1, h, 128, 384, 0), (k0 + 3, h, 384, 128, 384)], [0, 384]))
        for h in range(0, QH, 2):
            banks.append(([(k0 + 2, h, 256, 256, 0), (k0 + 2, h + 1, 256, 256, 256)], [0, 256]))
        for kb in reversed(range(k0)):
            for h in range(QH):
                banks.append(([(kb, h, 0, 512, 0)], []))
        out.append((qt, banks))
    return out


def score_groups():
    pairs = {3: 2, 2: 3, 1: 1, 0: 2}
    groups = []
    for qt, banks in score_banks():
        n = pairs[qt]
        cuts = [3] * ((len(banks) - 2 * n) // 3) + [2] * n
        assert sum(cuts) == len(banks)
        at_ = 0
        for i, c in enumerate(cuts):
            groups.append((qt, banks[at_:at_ + c], i == len(cuts) - 1))
            at_ += c
    return groups


GROUPS = score_groups()
NGR = len(GROUPS)
NPB = 4
assert NGR % NPB == 0
HAS_TRI = [any(tri for _, tri in banks) for _, banks, _ in GROUPS]
NMASK = sum(HAS_TRI)
LAST = {qt: i for i, (qt, _, ends) in enumerate(GROUPS) if ends}


def build(nc, x, wq, wk, wv, wo, qw, kw, cos, sin, w1t, w1s, w2t, w2s, h1t, h1s, h2t, h2s, w3t, w3s, out):
    with ExitStack() as top:
        passed = top.enter_context(nc.semaphore("passed"))

        def dram(name, shape):
            return nc.dram_tensor(name, shape, F32, kind="Internal").ap()

        qk_parts = dram("qk_parts", [2, 2, B, H * HD, T])
        neg_max = dram("neg_max", [B * H, T])
        attn_t = dram("attn_t", [B, H * HD, T])
        x2_s = dram("x2_s", [NT, P, D])
        xf_t = dram("xf_t", [D, B * T])

        def sb(name, shape, dt=F32, ctx=top):
            return ctx.enter_context(nc.sbuf_tensor(name, shape, dt))

        X = sb("X", [P, NT, D])
        ident = sb("ident", [P, P])
        vres = sb("vres", [P, NU, TPB, QH * HD])

        prep(nc, sb, passed, X, ident, vres, x, wq, wk, wv, qw, kw, cos, sin, qk_parts)
        rowmax(nc, sb, passed, ident, qk_parts, neg_max)
        attention(nc, sb, passed, vres, qk_parts, neg_max, attn_t)
        mix(nc, sb, passed, X, ident, wo, attn_t, x2_s, xf_t)
    with ExitStack() as top:
        passed = top.enter_context(nc.semaphore("passed_ffn"))

        def sb(name, shape, dt=F32, ctx=top):
            return ctx.enter_context(nc.sbuf_tensor(name, shape, dt))
        ffn(nc, sb, passed, w1t, w1s, w2t, w2s, h1t, h1s, h2t, h2s, w3t, w3s, x2_s, xf_t, out)


def prep(nc, sb, passed, X, ident, vres, x, wq, wk, wv, qw, kw, cos, sin, qk_parts):
    with ExitStack() as ctx:
        def s_(name, shape, dt=F32):
            return sb(name, shape, dt, ctx)

        def ps(name, shape):
            return ctx.enter_context(nc.psum_tensor(name, shape, F32))

        def sem(name):
            return ctx.enter_context(nc.semaphore(name))

        W = s_("W", [P, DC, 3 * D])
        C = s_("C", [P, TPB, HD // 2])
        S = s_("S", [P, TPB, HD // 2])
        nw = s_("nw", [P, 2, HD])
        nw_raw = s_("nw_raw", [P, 2, HD])
        T1 = s_("T1", [P, TPB, 2, HD])
        T2 = s_("T2", [P, TPB, 2, HD])
        stats = s_("stats", [P, NT, 6])
        mv = s_("mv", [P, NT, 2])
        std = s_("std", [P, NT])
        rstd = s_("rstd", [P, NT])
        xn = s_("xn", [P, 2, D])
        xnT = s_("xnT", [P, 2, DC, P])
        sq = s_("sq", [P, 2, 2 * D])
        ms = s_("ms", [P, 2, 2 * H])
        rms = s_("rms", [P, 2, 2 * H])
        ri = s_("ri", [P, 2, 2 * H])
        ra = s_("ra", [P, 2, 2 * D])
        rb = s_("rb", [P, 2, 2 * D])
        rc = s_("rc", [P, 2, 2 * D])
        rd = s_("rd", [P, 2, 2 * D])
        hi = s_("hi", [P, 2, 4, 2 * P], F32R)
        lo = s_("lo", [P, 2, 4, 2 * P], F32R)
        p_tp = [ps(f"p_tp{i}", [P, DC, P]) for i in range(2)]
        p_qk = [ps(f"p_qk{i}", [P, 2 * D]) for i in range(2)]
        p_v = [ps(f"p_v{i}", [P, D]) for i in range(2)]
        p_tq = [ps(f"p_tq{i}", [P, 4, P]) for i in range(2)]

        x_in = [sem(f"x_in{i}") for i in range(4)]
        w_in = sem("w_in")
        tab_in = sem("tab_in")
        ident_ready = sem("ident_ready")
        dve_step = sem("dve_step")
        var_ready = sem("var_ready")
        std_ready = sem("std_ready")
        xn_ready = sem("xn_ready")
        xt_ready = sem("xt_ready")
        xnT_ready = sem("xnT_ready")
        qkv_ready = sem("qkv_ready")
        sq_ready = sem("sq_ready")
        v_ready = sem("v_ready")
        reduced = sem("reduced")
        ms_ready = sem("ms_ready")
        rms_ready = sem("rms_ready")
        rb_ready = sem("rb_ready")
        ri_ready = sem("ri_ready")
        rc_ready = sem("rc_ready")
        rd_ready = sem("rd_ready")
        tq_ready = sem("tq_ready")
        hi_ready = sem("hi_ready")
        lo_ready = sem("lo_ready")
        parts_out = [sem(f"parts_out{i}") for i in range(2)]

        xv = x.rearrange("(t p) d -> p t d", p=P)
        with nc.Block() as block:
            @block.sync
            def _(sp):
                for i in range(4):
                    n = NT // 4
                    sp.dma_start(X[:, i * n:(i + 1) * n, :], xv[:, i * n:(i + 1) * n, :]).then_inc(x_in[i], 16)
                    if i == 0:
                        for j, w in enumerate((wq, wk, wv)):
                            sp.dma_start(W[:, :, j * D:(j + 1) * D],
                                         w.rearrange("(c p) n -> p c n", p=P)).then_inc(w_in, 16)
                        sp.dma_start(C[:], cos.rearrange("(t p) d -> p t d", p=P)).then_inc(tab_in, 16)
                        sp.dma_start(S[:], sin.rearrange("(t p) d -> p t d", p=P)).then_inc(tab_in, 16)
                        sp.dma_start(nw_raw[:, 0, :], qw.partition_broadcast(P)).then_inc(tab_in, 16)
                        sp.dma_start(nw_raw[:, 1, :], kw.partition_broadcast(P)).then_inc(tab_in, 16)
                with sp.Fori(0, NG) as it:
                    for s in range(2):
                        for part, (buf, ready) in enumerate(((hi, hi_ready), (lo, lo_ready))):
                            sp.wait_ge(ready, at(it, TG, 2 * s + 2))
                            for qk in range(2):
                                dst = qk_parts[part, qk, it // (NG // B)].rearrange("(c p) t -> p c t", p=P)[
                                    :, :, bass.ds((it % (NG // B)) * TG * P + 2 * s * P, 2 * P)]
                                sp.dma_start(dst, buf[:, s, 2 * qk:2 * qk + 2, :].bitcast(F32)).then_inc(
                                    parts_out[s], 16)
                for s in range(2):
                    sp.wait_ge(parts_out[s], NG * 4 * 16)

            @block.gpsimd
            def _(pool):
                pool.memset(ident[:], 0.0).then_inc(ident_ready, 1)
                pool.wait_ge(ident_ready, 1)
                pool.affine_select(out=ident[:], in_=ident[:], compare_op=ALU.not_equal, fill=1.0, base=0,
                                   pattern=[[-1, P]], channel_multiplier=1).then_inc(ident_ready, 1)

                def body(it, first, last):
                    for j in range(TG):
                        s = j % 2
                        pool.wait_ge(rb_ready, at(it, TG, j + 1))
                        pool.tensor_tensor(rc[:, s, :], ra[:, s, :], rb[:, s, :], ALU.add).then_inc(rc_ready, 1)
                        pool.wait_ge(rc_ready, at(it, TG, j + 1))
                        pool.wait_ge(ri_ready, at(it, TG, j + 1))
                        wait(pool, tq_ready, at(it, TG, j - 1))
                        pool.tensor_tensor(rd[:, s, :].rearrange("p (g d) -> p g d", d=HD),
                                           rc[:, s, :].rearrange("p (g d) -> p g d", d=HD),
                                           ri[:, s, :].unsqueeze(2).to_broadcast([P, 2 * H, HD]),
                                           ALU.mult).then_inc(rd_ready, 1)
                peeled(pool, NG, body)

            @block.scalar
            def _(act):
                act.wait_ge(var_ready, 1)
                nc.scalar.activation(std[:], mv[:, :, 1], ACT.Sqrt).then_inc(std_ready, 1)

                def put_xnT(it, j):
                    s = j % 2
                    act.wait_ge(xt_ready, at(it, TG, j + 1))
                    wait(act, qkv_ready, at(it, TG, j - 1))
                    nc.scalar.copy(xnT[:, s], p_tp[s][:]).then_inc(xnT_ready, 1)

                def put_hi(it, j):
                    s, h = j % 2, j // 2
                    act.wait_ge(tq_ready, at(it, TG, j + 1))
                    wait(act, parts_out[h], at(it, 64, 0))
                    nc.scalar.copy(hi[:, h, :, (j % 2) * P:(j % 2 + 1) * P], p_tq[s][:]).then_inc(hi_ready, 1)

                def body(it, first, last):
                    for j in range(TG):
                        s = j % 2
                        act.wait_ge(qkv_ready, at(it, TG, j + 1))
                        wait(act, ms_ready, at(it, TG, j - 1))
                        nc.scalar.activation(sq[:, s, :], p_qk[s][:], ACT.Square).then_inc(sq_ready, 1)
                        nc.scalar.copy(
                            vres[:, bass.ds((it // (NG // B)) * (H // QH), H // QH),
                                 (it % (NG // B)) * TG + j, :],
                            p_v[s][:].rearrange("p (u e) -> p u e", e=QH * HD)).then_inc(v_ready, 1)
                        if not (last and j == TG - 1):
                            put_xnT(it, j + 1) if j < TG - 1 else put_xnT(it + 1, 0)
                        act.wait_ge(ms_ready, at(it, TG, j + 1))
                        wait(act, ri_ready, at(it, TG, j - 1))
                        nc.scalar.activation(rms[:, s, :], ms[:, s, :], ACT.Sqrt).then_inc(rms_ready, 1)
                        if not (first and j == 0):
                            put_hi(it, j - 1) if j else put_hi(it - 1, TG - 1)
                put_xnT(0, 0)
                peeled(act, NG, body)
                put_hi(NG - 1, TG - 1)

            @block.vector
            def _(dve):
                for i in range(4):
                    n = NT // 4
                    dve.wait_ge(x_in[i], 16)
                    for t in range(i * n, (i + 1) * n):
                        nc.vector.bn_stats(stats[:, t, :], X[:, t, :]).then_inc(dve_step, 1)
                for t in range(NT):
                    if t == 0:
                        dve.wait_ge(dve_step, NT)
                    nc.vector.bn_aggr(mv[:, t, :], stats[:, t, :]).then_inc(dve_step, 1)
                dve.wait_ge(dve_step, 2 * NT)
                nc.vector.tensor_scalar(mv[:, :, 1], mv[:, :, 1], LN_EPS, None, ALU.add).then_inc(var_ready, 1)
                step = Chain(dve, passed, dve_step, 2 * NT)
                dve.wait_ge(tab_in, 64)
                step(nc.vector.tensor_scalar(nw[:, 0, :], nw_raw[:, 0, :], HD ** -0.5, None, ALU.mult))
                step(nc.vector.tensor_copy(nw[:, 1, :], nw_raw[:, 1, :]))
                half = HD // 2
                for qk in range(2):
                    for a in range(2):
                        own = nw[:, qk, a * half:(a + 1) * half].unsqueeze(1).to_broadcast([P, TPB, half])
                        other = nw[:, qk, (1 - a) * half:(2 - a) * half].unsqueeze(1).to_broadcast([P, TPB, half])
                        dst = slice(a * half, (a + 1) * half)
                        step(nc.vector.tensor_tensor(T1[:, :, qk, dst], C[:], own, ALU.mult))
                        step(nc.vector.scalar_tensor_tensor(out=T2[:, :, qk, dst], in0=S[:],
                                                            scalar=1.0 if a else -1.0, in1=other,
                                                            op0=ALU.mult, op1=ALU.mult))
                dve.wait_ge(std_ready, 1)
                step(nc.vector.reciprocal(rstd[:], std[:]))

                def put_xn(it, j):
                    s, t = j % 2, it * TG + j
                    wait(dve, xt_ready, at(it, TG, j - 1))
                    nc.vector.tensor_scalar(xn[:, s, :], X[:, t, :], mv[:, t, 0:1], rstd[:, bass.ds(t, 1)],
                                            ALU.subtract, ALU.mult).then_inc(xn_ready, 1)

                def put_lo(it, j):
                    s, h = j % 2, j // 2
                    dve.wait_ge(hi_ready, at(it, TG, j + 1))
                    wait(dve, parts_out[h], at(it, 64, 0))
                    nc.vector.tensor_tensor(lo[:, h, :, (j % 2) * P:(j % 2 + 1) * P], p_tq[s][:],
                                            hi[:, h, :, (j % 2) * P:(j % 2 + 1) * P].bitcast(F32),
                                            ALU.subtract).then_inc(lo_ready, 1)

                def body(it, first, last):
                    for j in range(TG):
                        s = j % 2
                        pos = (it % (NG // B)) * TG + j
                        dve.wait_ge(sq_ready, at(it, TG, j + 1))
                        wait(dve, rms_ready, at(it, TG, j - 1))
                        nc.vector.tensor_reduce(ms[:, s, :], sq[:, s, :].rearrange("p (g d) -> p g d", d=HD),
                                                AX.X, ALU.add).then_inc(reduced, 1)
                        dve.wait_ge(reduced, at(it, TG, j + 1))
                        nc.vector.tensor_scalar(ms[:, s, :], ms[:, s, :], 1.0 / HD, RMS_EPS,
                                                ALU.mult, ALU.add).then_inc(ms_ready, 1)
                        wait(dve, rc_ready, at(it, TG, j - 1))
                        qk4 = p_qk[s][:].rearrange("p (k h d) -> p k h d", k=2, d=HD)
                        ra4 = ra[:, s, :].rearrange("p (k h d) -> p k h d", k=2, d=HD)
                        rb4 = rb[:, s, :].rearrange("p (k h d) -> p k h d", k=2, d=HD)
                        for k in range(2):
                            nc.vector.tensor_tensor(ra4[:, k], qk4[:, k],
                                                    T1[:, pos, k, :].unsqueeze(1).to_broadcast([P, H, HD]),
                                                    ALU.mult)
                        for k in range(2):
                            for a in range(2):
                                ins = nc.vector.tensor_tensor(
                                    rb4[:, k, :, a * half:(a + 1) * half],
                                    qk4[:, k, :, (1 - a) * half:(2 - a) * half],
                                    T2[:, pos, k, a * half:(a + 1) * half].unsqueeze(1).to_broadcast([P, H, half]),
                                    ALU.mult)
                        ins.then_inc(rb_ready, 1)
                        if not (last and j == TG - 1):
                            put_xn(it, j + 1) if j < TG - 1 else put_xn(it + 1, 0)
                        dve.wait_ge(rms_ready, at(it, TG, j + 1))
                        wait(dve, rd_ready, at(it, TG, j - 1))
                        nc.vector.reciprocal(ri[:, s, :], rms[:, s, :]).then_inc(ri_ready, 1)
                        if not (first and j == 0):
                            put_lo(it, j - 1) if j else put_lo(it - 1, TG - 1)
                put_xn(0, 0)
                peeled(dve, NG, body)
                put_lo(NG - 1, TG - 1)

            @block.tensor
            def _(pe):
                pe.wait_ge(ident_ready, 2)

                def turn_x(it, j):
                    s = j % 2
                    pe.wait_ge(xn_ready, at(it, TG, j + 1))
                    wait(pe, xnT_ready, at(it, TG, j - 1))
                    for c in range(DC):
                        ins = pe.transpose(p_tp[s][:, c, :], xn[:, s, c * P:(c + 1) * P], ident[:])
                    ins.then_inc(xt_ready, 1)

                def turn_qk(it, j):
                    s = j % 2
                    pe.wait_ge(rd_ready, at(it, TG, j + 1))
                    wait(pe, lo_ready, at(it, TG, j - 1))
                    for c in range(4):
                        ins = pe.transpose(p_tq[s][:, c, :], rd[:, s, c * P:(c + 1) * P], ident[:])
                    ins.then_inc(tq_ready, 1)

                def body(it, first, last):
                    for j in range(TG):
                        s = j % 2
                        pe.wait_ge(xnT_ready, at(it, TG, j + 1))
                        wait(pe, rb_ready, at(it, TG, j - 1))
                        for c in range(DC):
                            pe.matmul(p_qk[s][:], xnT[:, s, c, :], W[:, c, 0:2 * D], start=(c == 0),
                                      stop=(c == DC - 1))
                        wait(pe, v_ready, at(it, TG, j - 1))
                        for c in range(DC):
                            ins = pe.matmul(p_v[s][:], xnT[:, s, c, :], W[:, c, 2 * D:3 * D], start=(c == 0),
                                            stop=(c == DC - 1))
                        ins.then_inc(qkv_ready, 1)
                        if not (last and j == TG - 1):
                            turn_x(it, j + 1) if j < TG - 1 else turn_x(it + 1, 0)
                        if not (first and j == 0):
                            turn_qk(it, j - 1) if j else turn_qk(it - 1, TG - 1)
                turn_x(0, 0)
                pe.wait_ge(w_in, 48)
                peeled(pe, NG, body)
                turn_qk(NG - 1, TG - 1)


def load_quad_piece(sp, qk_parts, neg_max, QT, KT, u, g, landed):
    b, quad = u // (H // QH), u % (H // QH)
    for side, rows in ((0, (0, 0, 1, 1)), (1, (0, 1, 0, 1))):
        for r, part in enumerate(rows):
            src = qk_parts[part, side, b].rearrange("(q h d) t -> q d h t", h=QH, d=HD)[
                quad, :, :, g * QW:(g + 1) * QW]
            dst = (QT, KT)[side][r * HD:(r + 1) * HD, :, g * QW:(g + 1) * QW].bitcast(F32)
            sp.dma_start(dst, src).then_inc(landed, 16)
    if neg_max is not None:
        src = neg_max.rearrange("(u o h) t -> u o h t", h=QH, o=1)[u, :, :, g * QW:(g + 1) * QW]
        sp.dma_start(QT[4 * HD:ROWS, :, g * QW:(g + 1) * QW].bitcast(F32), src).then_inc(landed, 16)


def rowmax(nc, sb, passed, ident, qk_parts, neg_max):
    with ExitStack() as ctx:
        def s_(name, shape, dt=F32):
            return sb(name, shape, dt, ctx)

        def sem(name):
            return ctx.enter_context(nc.semaphore(name))

        QT = s_("QTm", [P, QH, T], F32R)
        KT = s_("KTm", [P, QH, T], F32R)
        ident_r = s_("ident_r", [P, P], F32R)
        future_f = s_("future_f", [P, P])
        future = s_("future", [P, P], F32R)
        mx = s_("mx", [P, QH * TPB])
        neg = s_("neg", [QH * TPB, P], F32R)
        p_s = [ctx.enter_context(nc.psum_tensor(f"p_s{i}", [P, T], F32)) for i in range(2)]
        loaded = sem("loaded")
        consts = sem("consts")
        consts_r = sem("consts_r")
        rows_ready = sem("rows_ready")
        rows_read = sem("rows_read")
        mx_ready = sem("mx_ready")
        turned = sem("turned")
        neg_ready = sem("neg_ready")
        neg_out = sem("neg_out")
        NR = QH * TPB
        NLOAD = 8 * NQT * 16

        with nc.Block() as block:
            @block.sync
            def _(sp):
                for g in range(NQT):
                    load_quad_piece(sp, qk_parts, None, QT, KT, 0, g, loaded)
                with sp.Fori(0, NU) as u:
                    wait_apart(sp, passed, turned, u + 1)
                    for g in range(NQT):
                        load_quad_piece(sp, qk_parts, None, QT, KT, (u + 1) % NU, g, loaded)
                    wait_apart(sp, passed, neg_ready, u + 1)
                    sp.dma_start(neg_max.rearrange("(u h) (t p) -> u (h t) p", h=QH, p=P)[u],
                                 neg[:].bitcast(F32)).then_inc(neg_out, 16)
                sp.wait_ge(neg_out, NU * 16)
                sp.wait_ge(loaded, (NU + 1) * NLOAD)

            @block.gpsimd
            def _(pool):
                pool.memset(future_f[:], 0.0).then_inc(consts, 1)
                pool.wait_ge(consts, 1)
                pool.affine_select(out=future_f[:], in_=future_f[:], compare_op=ALU.is_ge, fill=MASKED, base=0,
                                   pattern=[[-1, P]], channel_multiplier=1).then_inc(consts, 1)

            @block.tensor
            def _(pe):
                pe.wait_ge(consts_r, 2)
                with pe.Fori(0, NU) as u:
                    pe.wait_ge(loaded, at(u, NLOAD, NLOAD))
                    for n in range(NR):
                        h, qb = n // TPB, n % TPB
                        buf = p_s[n % 2]
                        pe.wait_ge(mx_ready, at(u, NR, n + 1))
                        keys = (qb + 1) * P
                        q = QT[0:4 * HD, h, qb * P:(qb + 1) * P]
                        for k0 in range(0, keys - P, QW):
                            k1 = min(k0 + QW, keys - P)
                            pe.matmul(buf[:, k0:k1], q, KT[0:4 * HD, h, k0:k1], start=True, stop=True)
                        pe.matmul(buf[:, keys - P:keys], q, KT[0:4 * HD, h, keys - P:keys], start=True, stop=False)
                        pe.matmul(buf[:, keys - P:keys], ident_r[:], future[:], start=False,
                                  stop=True).then_inc(rows_ready, 1)
                    wait_apart(pe, passed, mx_ready, at(u, NR, NR + 2))
                    pe.transpose(p_s[0][0:NR, 0:P], mx[:], ident[:]).then_inc(turned, 1)
                    pe.wait_ge(neg_ready, u + 1)

            @block.vector
            def _(dve):
                dve.wait_ge(consts, 2)
                nc.vector.tensor_copy(future[:], future_f[:]).then_inc(consts_r, 1)
                nc.vector.tensor_copy(ident_r[:], ident[:]).then_inc(consts_r, 1)
                dve.nop().then_inc(mx_ready, 2)
                with dve.Fori(0, NU) as u:
                    for n in range(NR):
                        keys = (n % TPB + 1) * P
                        dve.wait_ge(rows_ready, at(u, NR, n + 1))
                        nc.vector.tensor_reduce(mx[:, n:n + 1], p_s[n % 2][:, 0:keys], AX.X,
                                                ALU.max).then_inc(mx_ready, 1)
                    dve.wait_ge(turned, u + 1)
                    nc.vector.tensor_scalar(neg[:], p_s[0][0:NR, 0:P], -1.0, None, ALU.mult).then_inc(neg_ready, 1)
                    dve.wait_ge(neg_out, at(u, 16, 16))


def attention(nc, sb, passed, vres, qk_parts, neg_max, attn_t):
    with ExitStack() as ctx:
        def s_(name, shape, dt=F32):
            return sb(name, shape, dt, ctx)

        def sem(name):
            return ctx.enter_context(nc.semaphore(name))

        QT = s_("QT", [P, QH, T], F32R)
        KT = s_("KT", [P, QH, T], F32R)
        V = s_("V", [P, TPB, QH, STRIP])
        probs = [s_(f"probs{i}", [P, 3 * QW]) for i in range(NPB)]
        o_sb = [s_(f"o_sb{i}", [P, QW]) for i in range(2)]
        den = s_("den", [P, QW])
        rden = s_("rden", [P, QW])
        o_norm = [s_(f"o_norm{i}", [P, QW]) for i in range(2)]
        p_s = [ctx.enter_context(nc.psum_tensor(f"p_sc{i}", [P, 3 * QW], F32)) for i in range(2)]
        p_o = [ctx.enter_context(nc.psum_tensor(f"p_o{i}", [P, QW], F32)) for i in range(2)]

        kq_in = [sem(f"kq_in{g}") for g in range(NQT)]
        ones_ready = sem("ones_ready")
        v_ones = sem("v_ones")
        v_in = sem("v_in")
        scores_ready = sem("scores_ready")
        probs_ready = sem("probs_ready")
        masked = sem("masked")
        probs_used = sem("probs_used")
        o_copied = sem("o_copied")
        den_ready = sem("den_ready")
        rden_ready = sem("rden_ready")
        o_ready = sem("o_ready")
        o_out = [sem(f"o_out{i}") for i in range(2)]
        NDMA = 9 * 16

        with nc.Block() as block:
            @block.sync
            def _(sp):
                for s in range(2):
                    sp.nop().then_inc(o_out[s], 64)
                for g in reversed(range(NQT)):
                    load_quad_piece(sp, qk_parts, neg_max, QT, KT, 0, g, kq_in[g])

                def body(u, last):
                    b, quad = u // (H // QH), u % (H // QH)
                    for i, g in enumerate(reversed(range(NQT))):
                        if not last:
                            wait_apart(sp, passed, scores_ready, at(u, NGR, LAST[g] + 1))
                            load_quad_piece(sp, qk_parts, neg_max, QT, KT, u + 1, g, kq_in[g])
                        wait_apart(sp, passed, o_ready, at(u, NQT, i + 1))
                        for h in range(QH):
                            sp.dma_start(attn_t[b].rearrange("(q h d) t -> q h d t", h=QH, d=HD)[
                                quad, h, :, g * QW:(g + 1) * QW],
                                o_norm[i % 2][h * STRIP:h * STRIP + HD, :]).then_inc(o_out[i % 2], 16)
                with sp.Fori(0, NU - 1) as u:
                    body(u, False)
                body(NU - 1, True)
                for s in range(2):
                    sp.wait_ge(o_out[s], (NU * NQT // 2 + 1) * 64)

            @block.gpsimd
            def _(pool):
                pool.memset(V[:], 1.0).then_inc(v_ones, 1)
                pool.wait_ge(v_ones, 1)

                def put_v(u, g):
                    nc.gpsimd.tensor_copy(V[:, g * KPQ:(g + 1) * KPQ, :, 0:HD],
                                          vres[:, u, g * KPQ:(g + 1) * KPQ, :].rearrange(
                                              "p k (h d) -> p k h d", d=HD)).then_inc(v_in, 1)

                for g in reversed(range(NQT)):
                    put_v(0, g)

                def mask(buf, kinds):
                    b0 = 0
                    while b0 < len(kinds):
                        tri, m = kinds[b0], b0 + 1
                        if len(tri) == 1:
                            while m < len(kinds) and kinds[m] == tri:
                                m += 1
                            v = buf[:, b0 * QW:m * QW].rearrange("p (n c) -> p n c", c=QW)[:, :, 0:P]
                        elif tri:
                            v = buf[:, b0 * QW:m * QW].rearrange("p (a c) -> p a c", c=P)[
                                :, 0:tri[1] // P + 1:tri[1] // P, :]
                        if tri:
                            ins = nc.gpsimd.affine_select(out=v, in_=v, compare_op=ALU.is_ge, fill=0.0, base=0,
                                                          pattern=[[0, v.shape[1]], [1, P]],
                                                          channel_multiplier=-1)
                        b0 = m
                    return ins

                def body(u, last):
                    n = 0
                    for i, (qt, banks, ends) in enumerate(GROUPS):
                        if HAS_TRI[i]:
                            n += 1
                            wait_apart(pool, passed, probs_ready, at(u, NGR, i + 1 + 2))
                            mask(probs[i % NPB], [tuple(tri) for _, tri in banks]).then_inc(masked, 1)
                            if not HAS_TRI[(i + 1) % NGR] or GROUPS[(i + 1) % NGR][0] != qt:
                                if not last and qt < NQT - 1:
                                    pool.wait_ge(probs_used, at(u, NGR, LAST[qt + 1] + 1 + NPB))
                                    put_v(u + 1, qt + 1)
                    if not last:
                        pool.wait_ge(probs_used, at(u, NGR, LAST[0] + 1 + NPB))
                        put_v(u + 1, 0)
                with pool.Fori(0, NU - 1) as u:
                    body(u, False)
                body(NU - 1, True)

            @block.scalar
            def _(act):
                act.nop().then_inc(probs_ready, 2)
                with act.Fori(0, NU) as u:
                    for i, (qt, banks, ends) in enumerate(GROUPS):
                        n = len(banks) * QW
                        act.wait_ge(scores_ready, at(u, NGR, i + 1))
                        act.wait_ge(probs_used, at(u, NGR, i + 1))
                        nc.scalar.activation(probs[i % NPB][:, 0:n], p_s[i % 2][:, 0:n],
                                             ACT.Exp).then_inc(probs_ready, 1)

            @block.tensor
            def _(pe):
                pe.nop().then_inc(probs_used, NPB)
                pe.wait_ge(ones_ready, 1)
                pe.wait_ge(v_ones, 1)

                def scores(u, i, pieces):
                    qt, banks, _ = GROUPS[i]
                    pe.wait_ge(probs_ready, at(u, NGR, i + 1))
                    for n, (items, _) in enumerate(banks):
                        for kb, h, q0, w, c in items:
                            g = kb // KPQ
                            if g not in pieces:
                                pieces.add(g)
                                pe.wait_ge(kq_in[g], at(u, NDMA, NDMA))
                            ins = pe.matmul(p_s[i % 2][:, n * QW + c:n * QW + c + w],
                                            KT[0:ROWS, h, kb * P:(kb + 1) * P],
                                            QT[0:ROWS, h, qt * QW + q0:qt * QW + q0 + w],
                                            start=True, stop=True)
                    ins.then_inc(scores_ready, 1)

                def values(u, i):
                    qt, banks, ends = GROUPS[i]
                    order = NQT - 1 - qt
                    if i == 0 or GROUPS[i - 1][0] != qt:
                        pe.wait_ge(o_copied, at(u, NQT, order + 1))
                    if qt == NQT - 1:
                        g = min(kb for items, _ in banks for kb, *_ in items) // KPQ
                        pe.wait_ge(v_in, at(u, NQT, NQT - g))
                    pe.wait_ge(probs_ready, at(u, NGR, i + 1 + 2))
                    if HAS_TRI[i]:
                        pe.wait_ge(masked, at(u, NMASK, sum(HAS_TRI[:i + 1])))
                    for n, (items, _) in enumerate(banks):
                        for kb, h, q0, w, c in items:
                            ins = pe.matmul(p_o[order % 2][h * STRIP:(h + 1) * STRIP, q0:q0 + w],
                                            V[:, kb, h, :], probs[i % NPB][:, n * QW + c:n * QW + c + w],
                                            start=(kb == KPQ * qt), stop=(kb == (0 if qt else 3)),
                                            skip_group_check=True)
                    ins.then_inc(probs_used, 1)

                with pe.Fori(0, NU) as u:
                    pieces = set()
                    scores(u, 0, pieces)
                    scores(u, 1, pieces)
                    for i in range(NGR):
                        if i + 2 < NGR:
                            scores(u, i + 2, pieces)
                        if i >= 1:
                            values(u, i - 1)
                    values(u, NGR - 1)

            @block.vector
            def _(dve):
                dve.memset(KT[4 * HD:ROWS, :, :].bitcast(F32), 1.0).then_inc(ones_ready, 1)
                dve.nop().then_inc(o_copied, 2)
                with dve.Fori(0, NU) as u:
                    for i, qt in enumerate(reversed(range(NQT))):
                        dve.wait_ge(probs_used, at(u, NGR, LAST[qt] + 1 + NPB))
                        nc.vector.tensor_copy(o_sb[i % 2][:], p_o[i % 2][:]).then_inc(o_copied, 1)
                        wait_apart(dve, passed, o_copied, at(u, NQT, i + 1 + 2))
                        nc.vector.stream_shuffle(den[:], o_sb[i % 2][:], [HD] * STRIP).then_inc(den_ready, 1)
                        dve.wait_ge(den_ready, at(u, NQT, i + 1))
                        nc.vector.reciprocal(rden[:], den[:]).then_inc(rden_ready, 1)
                        dve.wait_ge(rden_ready, at(u, NQT, i + 1))
                        dve.wait_ge(o_out[i % 2], at(u, 128, 64 * (i // 2) + 64))
                        nc.vector.tensor_tensor(o_norm[i % 2][:], o_sb[i % 2][:], rden[:], ALU.mult).then_inc(o_ready, 1)


def mix(nc, sb, passed, X, ident, wo, attn_t, x2_s, xf_t):
    with ExitStack() as ctx:
        def s_(name, shape, dt=F32):
            return sb(name, shape, dt, ctx)

        def sem(name):
            return ctx.enter_context(nc.semaphore(name))

        Wo = s_("Wo", [P, DC, D])
        at_in = s_("at_in", [P, DC, QW])
        st = s_("st", [P, 2, TG, 6])
        mv = s_("mv2", [P, 2, TG, 2])
        sd = s_("sd", [P, 2, TG])
        rs = s_("rs", [P, 2, TG])
        t1 = s_("t1", [P, TG, D])
        x2 = s_("x2", [P, TG, D])
        xf = s_("xf", [P, TG, D])
        xfT = s_("xfT", [P, DC, QW])
        p_y = [ctx.enter_context(nc.psum_tensor(f"p_y{j}", [P, D], F32)) for j in range(TG)]
        p_x = [ctx.enter_context(nc.psum_tensor(f"p_x{j}", [P, DC, P], F32)) for j in range(TG)]
        wo_in = sem("wo_in")
        attn_in = sem("attn_in")
        y_ready = sem("y_ready")
        step_m = sem("step_m")
        var_ready = sem("var_m")
        std_ready = sem("std_m")
        xf_ready = sem("xf_ready")
        xt_ready = sem("xt_m")
        xfT_ready = sem("xfT_ready")
        stored = sem("stored")
        X2_STEP = TG + TG + 1 + TG + TG
        NCH = X2_STEP + TG + TG + 1

        with nc.Block() as block:
            @block.sync
            def _(sp):
                sp.nop().then_inc(stored, 32)
                sp.dma_start(Wo[:], wo.rearrange("(c p) n -> p c n", p=P)).then_inc(wo_in, 16)

                def load(g):
                    sp.dma_start(at_in[:], attn_t[g // (NG // B)].rearrange("(c p) t -> p c t", p=P)[
                        :, :, bass.ds((g % (NG // B)) * QW, QW)]).then_inc(attn_in, 16)
                load(0)
                with sp.Fori(0, NG) as it:
                    wait_apart(sp, passed, y_ready, at(it, TG, TG))
                    load((it + 1) % NG)
                    wait_apart(sp, passed, step_m, at(it, NCH, X2_STEP))
                    sp.dma_start(x2_s.rearrange("(g t) p d -> g p t d", t=TG)[it], x2[:]).then_inc(stored, 16)
                    wait_apart(sp, passed, xfT_ready, at(it, TG, TG))
                    sp.dma_start(xf_t.rearrange("(c p) t -> p c t", p=P)[:, :, bass.ds(it * QW, QW)],
                                 xfT[:]).then_inc(stored, 16)
                sp.wait_ge(stored, (NG + 1) * 32)
                sp.wait_ge(attn_in, (NG + 1) * 16)

            @block.tensor
            def _(pe):
                pe.wait_ge(wo_in, 16)
                with pe.Fori(0, NG) as it:
                    pe.wait_ge(attn_in, at(it, 16, 16))
                    for j in range(TG):
                        for c in range(DC):
                            ins = pe.matmul(p_y[j][:], at_in[:, c, j * P:(j + 1) * P], Wo[:, c, :],
                                            start=(c == 0), stop=(c == DC - 1))
                        ins.then_inc(y_ready, 1)
                    pe.wait_ge(xf_ready, it + 1)
                    for j in range(TG):
                        for c in range(DC):
                            ins = pe.transpose(p_x[j][:, c, :], xf[:, j, c * P:(c + 1) * P], ident[:])
                        ins.then_inc(xt_ready, 1)

            @block.scalar
            def _(act):
                with act.Fori(0, NG) as it:
                    for k in range(2):
                        act.wait_ge(var_ready, at(it, 2, k + 1))
                        nc.scalar.activation(sd[:, k], mv[:, k, :, 1], ACT.Sqrt).then_inc(std_ready, 1)
                    act.wait_ge(stored, at(it, 32, 32))
                    for j in range(TG):
                        act.wait_ge(xt_ready, at(it, TG, j + 1))
                        nc.scalar.copy(xfT[:, :, j * P:(j + 1) * P], p_x[j][:]).then_inc(xfT_ready, 1)

            @block.vector
            def _(dve):
                with dve.Fori(0, NG) as it:
                    step = Chain(dve, passed, step_m, at(it, NCH, 0))
                    for j in range(TG):
                        dve.wait_ge(y_ready, at(it, TG, j + 1))
                        step(nc.vector.bn_stats(st[:, 0, j], p_y[j][:]))
                    for j in range(TG):
                        step(nc.vector.bn_aggr(mv[:, 0, j], st[:, 0, j]))
                    nc.vector.tensor_scalar(mv[:, 0, :, 1], mv[:, 0, :, 1], LN_EPS, None,
                                            ALU.add).then_inc(var_ready, 1)
                    dve.wait_ge(std_ready, at(it, 2, 1))
                    step(nc.vector.reciprocal(rs[:, 0], sd[:, 0]))
                    for j in range(TG):
                        step(nc.vector.tensor_scalar(t1[:, j], p_y[j][:], mv[:, 0, j, 0:1], rs[:, 0, j:j + 1],
                                                     ALU.subtract, ALU.mult))
                    dve.wait_ge(stored, at(it, 32, 32))
                    for j in range(TG):
                        step(nc.vector.tensor_tensor(x2[:, j], t1[:, j], X[:, it * TG + j], ALU.add))
                    assert step.n == X2_STEP
                    for j in range(TG):
                        step(nc.vector.bn_stats(st[:, 1, j], x2[:, j]))
                    for j in range(TG):
                        step(nc.vector.bn_aggr(mv[:, 1, j], st[:, 1, j]))
                    nc.vector.tensor_scalar(mv[:, 1, :, 1], mv[:, 1, :, 1], LN_EPS, None,
                                            ALU.add).then_inc(var_ready, 1)
                    dve.wait_ge(std_ready, at(it, 2, 2))
                    step(nc.vector.reciprocal(rs[:, 1], sd[:, 1]))
                    assert step.n == NCH
                    for j in range(TG):
                        ins = nc.vector.tensor_scalar(xf[:, j], x2[:, j], mv[:, 1, j, 0:1], rs[:, 1, j:j + 1],
                                                      ALU.subtract, ALU.mult)
                    ins.then_inc(xf_ready, 1)


def ffn(nc, sb, passed, w1t, w1s, w2t, w2s, h1t, h1s, h2t, h2s, w3t, w3s, x2_s, xf_t, out):
    with ExitStack() as ctx:
        def s_(name, shape, dt=F32):
            return sb(name, shape, dt, ctx)

        def sem(name):
            return ctx.enter_context(nc.semaphore(name))

        W1 = s_("W1", [P, DC, HID])
        W2 = s_("W2", [P, DC, HID])
        H1 = s_("H1", [P, HC, HID])
        H2 = s_("H2", [P, HC, HID])
        W3 = s_("W3", [P, HC, D])
        S = s_("Sc", [P, 4, HC])
        S3 = s_("S3", [P, D])
        xfT = s_("xfT_in", [P, DC, QW])
        x2 = s_("x2_in", [P, TG, D])
        gate = [s_(f"gate{i}", [P, QW]) for i in range(2)]
        ha = s_("ha", [P, HC, QW])
        hb = s_("hb", [P, HC, QW])
        y = s_("y", [P, TG, D])
        st = s_("st3", [P, TG, 6])
        mv = s_("mv3", [P, TG, 2])
        sd = s_("sd3", [P, TG])
        rs = s_("rs3", [P, TG])
        o1 = s_("o1", [P, TG, D])
        ob = s_("ob", [P, TG, D])
        NBK = 6
        USES = 2 * HC + HC + HC + TG
        assert USES % NBK == 0
        bank = [ctx.enter_context(nc.psum_tensor(f"bank{i}", [P, QW], F32)) for i in range(NBK)]
        w_in = [sem(f"w_in{i}") for i in range(4)]
        xf_in = sem("xf_in")
        x2_in = sem("x2_in_s")
        pe_ready = sem("pe_ready")
        gate_ready = sem("gate_ready")
        h1_ready = sem("h1_ready")
        h23_ready = sem("h23_ready")
        y_ready = sem("y3_ready")
        step_f = sem("step_f")
        var_ready = sem("var_f")
        std_ready = sem("std_f")
        ob_ready = sem("ob_ready")
        out_done = sem("out_done")
        NCH = TG + TG + 1 + TG
        ov = out.rearrange("(g t p) d -> g p t d", t=TG, p=P)

        with nc.Block() as block:
            @block.sync
            def _(sp):
                sp.nop().then_inc(out_done, 16)
                for i, (w, s) in enumerate(((w1s, 0), (w2s, 1), (h1s, 2), (h2s, 3))):
                    sp.dma_start(S[:, i, :], w).then_inc(w_in[0], 16)
                sp.dma_start(S3[:], w3s.partition_broadcast(P)).then_inc(w_in[0], 16)

                def load_xf(g):
                    sp.dma_start(xfT[:], xf_t.rearrange("(c p) t -> p c t", p=P)[:, :, bass.ds(g * QW, QW)]
                                 ).then_inc(xf_in, 16)

                def load_x2(g):
                    sp.dma_start(x2[:], x2_s.rearrange("(g t) p d -> g p t d", t=TG)[g]).then_inc(x2_in, 16)
                load_xf(0)
                sp.dma_start(W1[:], w1t.rearrange("(c p) n -> p c n", p=P)).then_inc(w_in[0], 16)
                sp.dma_start(W2[:], w2t.rearrange("(c p) n -> p c n", p=P)).then_inc(w_in[0], 16)
                sp.dma_start(H1[:], h1t.rearrange("(c p) n -> p c n", p=P)).then_inc(w_in[1], 16)
                sp.dma_start(H2[:], h2t.rearrange("(c p) n -> p c n", p=P)).then_inc(w_in[2], 16)
                sp.dma_start(W3[:], w3t.rearrange("(c p) n -> p c n", p=P)).then_inc(w_in[3], 16)
                load_x2(0)
                with sp.Fori(0, NG) as it:
                    wait_apart(sp, passed, pe_ready, at(it, USES, 2 * HC))
                    load_xf((it + 1) % NG)
                    wait_apart(sp, passed, ob_ready, it + 1)
                    sp.dma_start(ov[it], ob[:]).then_inc(out_done, 16)
                    load_x2((it + 1) % NG)
                sp.wait_ge(out_done, (NG + 1) * 16)
                sp.wait_ge(xf_in, (NG + 1) * 16)
                sp.wait_ge(x2_in, (NG + 1) * 16)

            @block.tensor
            def _(pe):
                pe.wait_ge(w_in[0], 7 * 16)
                for i in range(1, 4):
                    pe.wait_ge(w_in[i], 16)

                def wait_read(it, n):
                    turn, n = (0, n) if n >= 0 else (-1, n + USES)
                    if n >= 4 * HC:
                        pe.wait_ge(y_ready, at(it, TG, TG + TG * turn + n - 4 * HC + 1))
                    elif n >= 2 * HC:
                        pe.wait_ge(h23_ready, at(it, 2 * HC, 2 * HC + 2 * HC * turn + n - 2 * HC + 1))
                    elif n % 2:
                        pe.wait_ge(h1_ready, at(it, HC, 2 + n // 2 + 1))
                    else:
                        pe.wait_ge(gate_ready, at(it, HC, n // 2 + 1))
                with pe.Fori(0, NG) as it:
                    n = 0

                    def use(width, pairs):
                        nonlocal n
                        b = n % NBK
                        wait_read(it, n - NBK)
                        for k, (w, m) in enumerate(pairs):
                            ins = pe.matmul(bank[b][:, 0:width], w, m, start=(k == 0), stop=(k == len(pairs) - 1))
                        ins.then_inc(pe_ready, 1)
                        n += 1
                    pe.wait_ge(xf_in, at(it, 16, 16))
                    for m in range(HC):
                        for W in (W1, W2):
                            use(QW, [(W[:, c, m * P:(m + 1) * P], xfT[:, c, :]) for c in range(DC)])
                    pe.wait_ge(h1_ready, at(it, HC, HC + 2))
                    for m in range(HC):
                        use(QW, [(H1[:, c, m * P:(m + 1) * P], ha[:, c, :]) for c in range(HC)])
                    pe.wait_ge(h23_ready, at(it, 2 * HC, 2 * HC + HC))
                    for m in range(HC):
                        use(QW, [(H2[:, c, m * P:(m + 1) * P], hb[:, c, :]) for c in range(HC)])
                    pe.wait_ge(h23_ready, at(it, 2 * HC, 2 * HC + 2 * HC))
                    for j in range(TG):
                        use(D, [(ha[:, c, j * P:(j + 1) * P], W3[:, c, :]) for c in range(HC)])

            @block.scalar
            def _(act):
                act.nop().then_inc(h23_ready, 2 * HC)
                act.wait_ge(w_in[0], 7 * 16)
                with act.Fori(0, NG) as it:
                    for m in range(HC):
                        n = 2 * m
                        act.wait_ge(pe_ready, at(it, USES, n + 1))
                        act.wait_ge(h1_ready, at(it, HC, m + 1))
                        ins = nc.scalar.activation(gate[m % 2][:], bank[n % NBK][:], ACT.Silu, scale=S[:, 0, m:m + 1])
                        ins.then_inc(gate_ready, 1)
                    for layer, dst in ((2, hb), (3, ha)):
                        for m in range(HC):
                            n = layer * HC + m
                            act.wait_ge(pe_ready, at(it, USES, n + 1))
                            nc.scalar.activation(dst[:, m, :], bank[n % NBK][:], ACT.Gelu,
                                                 scale=S[:, layer, m:m + 1]).then_inc(h23_ready, 1)
                    act.wait_ge(var_ready, it + 1)
                    nc.scalar.activation(sd[:], mv[:, :, 1], ACT.Sqrt).then_inc(std_ready, 1)

            @block.vector
            def _(dve):
                dve.nop().then_inc(h1_ready, 2)
                dve.nop().then_inc(y_ready, TG)
                dve.wait_ge(w_in[0], 7 * 16)
                with dve.Fori(0, NG) as it:
                    for m in range(HC):
                        n = 2 * m + 1
                        dve.wait_ge(pe_ready, at(it, USES, n + 1))
                        dve.wait_ge(gate_ready, at(it, HC, m + 1))
                        nc.vector.scalar_tensor_tensor(out=ha[:, m, :], in0=bank[n % NBK][:], scalar=S[:, 1, m:m + 1],
                                                       in1=gate[m % 2][:], op0=ALU.mult,
                                                       op1=ALU.mult).then_inc(h1_ready, 1)
                    step = Chain(dve, passed, step_f, at(it, NCH, 0))
                    for j in range(TG):
                        n = 4 * HC + j
                        dve.wait_ge(pe_ready, at(it, USES, n + 1))
                        nc.vector.tensor_tensor(y[:, j], bank[n % NBK][:, 0:D], S3[:], ALU.mult).then_inc(y_ready, 1)
                        dve.wait_ge(y_ready, at(it, TG, TG + j + 1))
                        step(nc.vector.bn_stats(st[:, j], y[:, j]))
                    for j in range(TG):
                        step(nc.vector.bn_aggr(mv[:, j], st[:, j]))
                    nc.vector.tensor_scalar(mv[:, :, 1], mv[:, :, 1], LN_EPS, None, ALU.add).then_inc(var_ready, 1)
                    dve.wait_ge(std_ready, it + 1)
                    step(nc.vector.reciprocal(rs[:], sd[:]))
                    for j in range(TG):
                        step(nc.vector.tensor_scalar(o1[:, j], y[:, j], mv[:, j, 0:1], rs[:, j:j + 1],
                                                     ALU.subtract, ALU.mult))
                    dve.wait_ge(x2_in, at(it, 16, 16))
                    dve.wait_ge(out_done, at(it, 16, 16))
                    assert step.n == NCH
                    for j in range(TG):
                        ins = nc.vector.tensor_tensor(ob[:, j], o1[:, j], x2[:, j], ALU.add)
                    ins.then_inc(ob_ready, 1)


def kernel(L0_attn_x, L0_attn_Wq, L0_attn_Wk, L0_attn_Wv, L0_attn_Wo, L0_attn_q_norm_w, L0_attn_k_norm_w,
           L0_ffn_w1_w, L0_ffn_w1_s, L0_ffn_w2_w, L0_ffn_w2_s, L0_ffn_h1_w, L0_ffn_h1_s, L0_ffn_h2_w,
           L0_ffn_h2_s, L0_ffn_w3_w, L0_ffn_w3_s):
    import concourse.bacc as bacc
    from concourse.bass_utils import run_bass_kernel_spmd

    def rows(w):
        return np.ascontiguousarray(np.asarray(w).T)

    def columns(s):
        return np.ascontiguousarray(np.asarray(s).reshape(HC, P).T)

    inv_freq = (1.0 / np.float32(10000.0) ** (np.arange(0, HD, 2, dtype=np.float32) / np.float32(HD)))
    angle = np.outer(np.arange(T, dtype=np.float32), inv_freq.astype(np.float32)).astype(np.float32)
    arrays = {
        "x": np.ascontiguousarray(np.asarray(L0_attn_x).reshape(B * T, D)),
        "wq": np.asarray(L0_attn_Wq), "wk": np.asarray(L0_attn_Wk), "wv": np.asarray(L0_attn_Wv),
        "wo": np.asarray(L0_attn_Wo), "qw": np.asarray(L0_attn_q_norm_w), "kw": np.asarray(L0_attn_k_norm_w),
        "cos": np.cos(angle), "sin": np.sin(angle),
        "w1t": rows(L0_ffn_w1_w), "w1s": columns(L0_ffn_w1_s), "w2t": rows(L0_ffn_w2_w), "w2s": columns(L0_ffn_w2_s),
        "h1t": rows(L0_ffn_h1_w), "h1s": columns(L0_ffn_h1_s), "h2t": rows(L0_ffn_h2_w), "h2s": columns(L0_ffn_h2_s),
        "w3t": rows(L0_ffn_w3_w), "w3s": np.asarray(L0_ffn_w3_s),
    }
    nc = bacc.Bacc("TRN2", target_bir_lowering=False, num_devices=1)
    args = [nc.dram_tensor(n, a.shape, mybir.dt.from_np(a.dtype), kind="ExternalInput").ap()
            for n, a in arrays.items()]
    out = nc.dram_tensor("out", (B * T, D), F32, kind="ExternalOutput").ap()
    build(nc, *args, out)
    r = run_bass_kernel_spmd(nc, [arrays], core_ids=[0])
    return r.results[0]["out"].reshape(B, T, D)
```

```python
from contextlib import ExitStack

import numpy as np
import concourse.bass as bass
from concourse import mybir

F32 = mybir.dt.float32
F32R = mybir.dt.float32r
I32 = mybir.dt.int32
ALU = mybir.AluOpType
ACT = mybir.ActivationFunctionType
AX = mybir.AxisListType

P = 128
B, T, D = 2, 2048, 256
H, HD = 16, 16
HID = 1024
NT = B * T // P
TPB = T // P
DC = D // P
HC = HID // P
QH = 4
NU = B * H // QH
QW = 512
NQT = T // QW
KPQ = QW // P
ROWS = 4 * HD + 1
STRIP = 32
LN_EPS = 1e-5
RMS_EPS = 1e-6
MASKED = -1e30
TG = 4
NG = NT // TG
MAX_SCORE = 40.0
W_CHUNK = 2048
W_CHUNKS = (2 * D * HID + 2 * HID * HID + HID * D) // P // W_CHUNK
W_KEPT = 8


class Shared:
    pass


class Arena:

    def __init__(self, nc, start):
        self.nc, self.at = nc, start

    def __call__(self, name, shape, dt=F32):
        t = self.nc.alloc_sbuf_tensor_at(name, shape, dt, offset=self.at)
        self.at += -(-4 * int(np.prod(shape[1:])) // 32) * 32
        return t


def at(it, per, n):
    return it * per + n


def wait(eng, sem, value):
    if not isinstance(value, int) or value > 0:
        eng.wait_ge(sem, value)


def wait_apart(eng, passed, sem, value):
    eng.wait_ge(sem, value)
    eng.sem_inc(passed, 1)


class Chain:

    def __init__(self, eng, passed, sem, base=0):
        self.eng, self.passed, self.sem, self.base, self.n = eng, passed, sem, base, 0

    def __call__(self, ins):
        self.n += 1
        ins.then_inc(self.sem, 1)
        wait_apart(self.eng, self.passed, self.sem, self.base + self.n)


def ahead(it, j):
    return (it + j // TG, j % TG)


def peeled(eng, n, body):
    body(0, True, False)
    with eng.Fori(1, n - 1) as it:
        body(it, False, False)
    body(n - 1, False, True)


def score_banks():
    out = []
    for qt in reversed(range(NQT)):
        banks, k0 = [], KPQ * qt
        for h in range(QH):
            banks.append(([(k0, h, 0, 512, 0)], [0]))
        for h in range(QH):
            banks.append(([(k0 + 1, h, 128, 384, 0), (k0 + 3, h, 384, 128, 384)], [0, 384]))
        for h in range(0, QH, 2):
            banks.append(([(k0 + 2, h, 256, 256, 0), (k0 + 2, h + 1, 256, 256, 256)], [0, 256]))
        for kb in reversed(range(k0)):
            for h in range(QH):
                banks.append(([(kb, h, 0, 512, 0)], []))
        out.append((qt, banks))
    return out


def score_groups():
    pairs = {3: 2, 2: 3, 1: 1, 0: 2}
    groups = []
    for qt, banks in score_banks():
        n = pairs[qt]
        cuts = [3] * ((len(banks) - 2 * n) // 3) + [2] * n
        assert sum(cuts) == len(banks)
        at_ = 0
        for i, c in enumerate(cuts):
            groups.append((qt, banks[at_:at_ + c], i == len(cuts) - 1))
            at_ += c
    return groups


GROUPS = score_groups()
NGR = len(GROUPS)
NPB = 3
assert NGR % NPB == 0
HAS_TRI = [any(tri for _, tri in banks) for _, banks, _ in GROUPS]
NMASK = sum(HAS_TRI)
FIRST = {}
for _i, (_qt, _banks, _) in enumerate(GROUPS):
    for _items, _ in _banks:
        FIRST.setdefault(_items[0][0] // KPQ, _i)
LAST = {qt: i for i, (qt, _, ends) in enumerate(GROUPS) if ends}


def build(nc, x, wq, wk, wv, wo, qw, kw, cos, sin, wffn, w1s, w2s, h1s, h2s, w3s, out):
    def dram(name, shape):
        return nc.dram_tensor(name, shape, F32, kind="Internal").ap()

    qk_parts = dram("qk_parts", [2, 2, B, H * HD, T])
    neg_max = dram("neg_max", [B * H, T])
    attn_t = dram("attn_t", [B, H * HD, T])
    x2_s = dram("x2_s", [NT, P, D])
    xf_t = dram("xf_t", [D, B * T])
    with ExitStack() as top:
        g = Shared()
        g.passed = top.enter_context(nc.semaphore("passed"))
        g.kq_in = [top.enter_context(nc.semaphore(f"kq_in{i}")) for i in range(NQT)]

        arena = Arena(nc, -(-nc.sbuf_base // 32) * 32)
        g.ident = arena("ident", [P, P])
        g.qk_small = arena("qk_small", [P, 1], I32)
        g.w_exact = arena("w_exact", [P, 1], I32)
        g.w_diff = arena("w_diff", [P, W_CHUNKS])
        weights_at = arena.at
        work_at = weights_at + W_KEPT * W_CHUNK * 4
        g.Wr = Arena(nc, weights_at)("Wr", [P, W_CHUNKS, W_CHUNK], F32R)
        g.Wf = Arena(nc, weights_at)("Wf", [P, W_CHUNKS, W_CHUNK])
        work = Arena(nc, work_at)
        g.QT = work("QT", [P, QH, T], F32R)
        g.KT = work("KT", [P, QH, T], F32R)
        g.V = work("V", [P, TPB, QH, STRIP])
        g.vres = work("vres", [P, NU, TPB, QH * HD])
        rest_at = work.at

        prep(nc, g, Arena(nc, weights_at), Arena(nc, rest_at), x, wq, wk, wv, qw, kw, cos, sin, qk_parts, neg_max)
        rowmax(nc, g, Arena(nc, weights_at), qk_parts, neg_max)
        attention(nc, g, Arena(nc, rest_at), wffn, qk_parts, neg_max, attn_t)
        after = Arena(nc, weights_at + W_CHUNKS * W_CHUNK * 4)
        mix(nc, g, after, x, wo, wffn, attn_t, x2_s, xf_t)
        ffn(nc, g, Arena(nc, weights_at + W_CHUNKS * W_CHUNK * 4), wffn, w1s, w2s, h1s, h2s, w3s, x2_s, xf_t, out)


def prep(nc, g, low, high, x, wq, wk, wv, qw, kw, cos, sin, qk_parts, neg_max):
    ident, vres, passed = g.ident, g.vres, g.passed
    with ExitStack() as ctx:
        s_ = high

        def ps(name, shape):
            return ctx.enter_context(nc.psum_tensor(name, shape, F32))

        def sem(name):
            return ctx.enter_context(nc.semaphore(name))

        X = low("X", [P, NT, D])
        shift = low("shift", [B * H, T])
        W = s_("W", [P, DC, 3 * D])
        C = s_("C", [P, TPB, HD // 2])
        S = s_("S", [P, TPB, HD // 2])
        nw = s_("nw", [P, 2, HD])
        nw_raw = s_("nw_raw", [P, 2, HD])
        T1 = s_("T1", [P, TPB, 2, HD])
        T2 = s_("T2", [P, TPB, 2, HD])
        stats = s_("stats", [P, NT, 6])
        mv = s_("mv", [P, NT, 2])
        std = s_("std", [P, NT])
        rstd = s_("rstd", [P, NT])
        xn = s_("xn", [P, 2, D])
        xnT = s_("xnT", [P, 2, DC, P])
        sq = s_("sq", [P, 2, 2 * D])
        ms = s_("ms", [P, 2, 2 * H])
        rms = s_("rms", [P, 2, 2 * H])
        ri = s_("ri", [P, 2, 2 * H])
        ra = s_("ra", [P, 2, 2 * D])
        rb = s_("rb", [P, 2, 2 * D])
        rc = s_("rc", [P, 2, 2 * D])
        rd = s_("rd", [P, 2, 2 * D])
        nmr = s_("nmr", [P, NT])
        w_max = s_("w_max", [P, 2])
        w_prod = s_("w_prod", [P, 1])
        hi = low("hi", [P, 2, 4, 2 * P], F32R)
        lo = low("lo", [P, 2, 4, 2 * P], F32R)
        p_tp = [ps(f"p_tp{i}", [P, DC, P]) for i in range(2)]
        p_qk = [ps(f"p_qk{i}", [P, 2 * D]) for i in range(2)]
        p_v = [ps(f"p_v{i}", [P, D]) for i in range(2)]
        p_tq = [ps(f"p_tq{i}", [P, 4, P]) for i in range(2)]

        x_in = [sem(f"x_in{i}") for i in range(4)]
        w_in = sem("w_in")
        tab_in = sem("tab_in")
        ident_ready = sem("ident_ready")
        zeros_ready = sem("zeros_ready")
        pads_ready = sem("pads_ready")
        dve_pad = sem("dve_pad")
        shift_ready = sem("shift_ready")
        shift_out = sem("shift_out")
        dve_step = sem("dve_step")
        norm_ready = sem("norm_ready")
        var_ready = sem("var_ready")
        std_ready = sem("std_ready")
        xn_ready = sem("xn_ready")
        xt_ready = sem("xt_ready")
        xnT_ready = sem("xnT_ready")
        qkv_ready = sem("qkv_ready")
        sq_ready = sem("sq_ready")
        v_ready = sem("v_ready")
        reduced = sem("reduced")
        ms_ready = sem("ms_ready")
        rms_ready = sem("rms_ready")
        rb_ready = sem("rb_ready")
        ri_ready = sem("ri_ready")
        rc_ready = sem("rc_ready")
        rd_ready = sem("rd_ready")
        tq_ready = sem("tq_ready")
        hi_ready = sem("hi_ready")
        lo_ready = sem("lo_ready")
        parts_out = [sem(f"parts_out{i}") for i in range(2)]

        xv = x.rearrange("(t p) d -> p t d", p=P)
        with nc.Block() as block:
            @block.sync
            def _(sp):
                for s in range(2):
                    sp.nop().then_inc(parts_out[s], 64)
                for i in range(4):
                    n = NT // 4
                    sp.dma_start(X[:, i * n:(i + 1) * n, :], xv[:, i * n:(i + 1) * n, :]).then_inc(x_in[i], 16)
                    if i == 0:
                        for j, w in enumerate((wq, wk, wv)):
                            sp.dma_start(W[:, :, j * D:(j + 1) * D],
                                         w.rearrange("(c p) n -> p c n", p=P)).then_inc(w_in, 16)
                        sp.dma_start(C[:], cos.rearrange("(t p) d -> p t d", p=P)).then_inc(tab_in, 16)
                        sp.dma_start(S[:], sin.rearrange("(t p) d -> p t d", p=P)).then_inc(tab_in, 16)
                        sp.dma_start(nw_raw[:, 0, :], qw.partition_broadcast(P)).then_inc(tab_in, 16)
                        sp.dma_start(nw_raw[:, 1, :], kw.partition_broadcast(P)).then_inc(tab_in, 16)
                sp.wait_ge(shift_ready, 1)
                sp.dma_start(neg_max, shift[:]).then_inc(shift_out, 16)

                def parts(it):
                    for s in range(2):
                        for part, (buf, ready) in enumerate(((hi, hi_ready), (lo, lo_ready))):
                            sp.wait_ge(ready, at(it, TG, 2 * s + 2))
                            for qk in range(2):
                                dst = qk_parts[part, qk, it // (NG // B)].rearrange("(c p) t -> p c t", p=P)[
                                    :, :, bass.ds((it % (NG // B)) * TG * P + 2 * s * P, 2 * P)]
                                sp.dma_start(dst, buf[:, s, 2 * qk:2 * qk + 2, :].bitcast(F32)).then_inc(
                                    parts_out[s], 16)
                with sp.Fori(0, NG // B) as it:
                    parts(it)
                for s in range(2):
                    sp.wait_ge(parts_out[s], (NG // B + 1) * 64)
                sp.wait_ge(pads_ready, 1)
                sp.wait_ge(dve_pad, 3)
                for piece in reversed(range(NQT)):
                    load_quad_piece(sp, qk_parts, g.QT, g.KT, 0, piece, g.kq_in[piece])
                with sp.Fori(NG // B, NG) as it:
                    parts(it)
                for s in range(2):
                    sp.wait_ge(parts_out[s], (NG + 1) * 64)
                sp.wait_ge(shift_out, 16)

            @block.gpsimd
            def _(pool):
                pool.memset(ident[:], 0.0).then_inc(ident_ready, 1)
                pool.wait_ge(ident_ready, 1)
                pool.affine_select(out=ident[:], in_=ident[:], compare_op=ALU.not_equal, fill=1.0, base=0,
                                   pattern=[[-1, P]], channel_multiplier=1).then_inc(ident_ready, 1)
                pool.memset(shift[:], 0.0).then_inc(zeros_ready, 1)
                pool.wait_ge(zeros_ready, 1)
                pool.memset(g.V[:], 1.0).then_inc(pads_ready, 1)

                def body(it, first, last):
                    for j in range(TG):
                        s = j % 2
                        pool.wait_ge(rb_ready, at(it, TG, j + 1))
                        pool.tensor_tensor(rc[:, s, :], ra[:, s, :], rb[:, s, :], ALU.add).then_inc(rc_ready, 1)
                        pool.wait_ge(rc_ready, at(it, TG, j + 1))
                        pool.wait_ge(ri_ready, at(it, TG, j + 1))
                        wait(pool, tq_ready, at(it, TG, j - 1))
                        pool.tensor_tensor(rd[:, s, :].rearrange("p (g d) -> p g d", d=HD),
                                           rc[:, s, :].rearrange("p (g d) -> p g d", d=HD),
                                           ri[:, s, :].unsqueeze(2).to_broadcast([P, 2 * H, HD]),
                                           ALU.mult).then_inc(rd_ready, 1)
                peeled(pool, NG, body)

            @block.scalar
            def _(act):
                act.wait_ge(var_ready, 1)
                nc.scalar.activation(std[:], mv[:, :, 1], ACT.Sqrt).then_inc(std_ready, 1)

                def put_xn(it, j):
                    s, t = j % 2, it * TG + j
                    wait(act, xt_ready, at(it, TG, j - 1))
                    nc.scalar.activation(xn[:, s, :], X[:, t, :], ACT.Identity, bias=nmr[:, bass.ds(t, 1)],
                                         scale=rstd[:, bass.ds(t, 1)]).then_inc(xn_ready, 1)

                def put_xnT(it, j):
                    s = j % 2
                    act.wait_ge(xt_ready, at(it, TG, j + 1))
                    wait(act, qkv_ready, at(it, TG, j - 1))
                    nc.scalar.copy(xnT[:, s], p_tp[s][:]).then_inc(xnT_ready, 1)

                def put_hi(it, j):
                    s, h = j % 2, j // 2
                    act.wait_ge(tq_ready, at(it, TG, j + 1))
                    act.wait_ge(parts_out[h], at(it, 64, 64))
                    nc.scalar.copy(hi[:, h, :, (j % 2) * P:(j % 2 + 1) * P], p_tq[s][:]).then_inc(hi_ready, 1)

                def body(it, first, last):
                    for j in range(TG):
                        s = j % 2
                        if not (last and j >= TG - 2):
                            put_xn(*ahead(it, j + 2))
                        if not (last and j == TG - 1):
                            put_xnT(*ahead(it, j + 1))
                        act.wait_ge(qkv_ready, at(it, TG, j + 1))
                        wait(act, ms_ready, at(it, TG, j - 1))
                        nc.scalar.activation(sq[:, s, :], p_qk[s][:], ACT.Square).then_inc(sq_ready, 1)
                        nc.scalar.copy(
                            vres[:, bass.ds((it // (NG // B)) * (H // QH), H // QH),
                                 (it % (NG // B)) * TG + j, :],
                            p_v[s][:].rearrange("p (u e) -> p u e", e=QH * HD)).then_inc(v_ready, 1)
                        act.wait_ge(ms_ready, at(it, TG, j + 1))
                        wait(act, ri_ready, at(it, TG, j - 1))
                        nc.scalar.activation(rms[:, s, :], ms[:, s, :], ACT.Sqrt).then_inc(rms_ready, 1)
                        if not (first and j < 2):
                            put_hi(*ahead(it, j - 2))
                act.wait_ge(norm_ready, 1)
                put_xn(0, 0)
                put_xn(0, 1)
                put_xnT(0, 0)
                peeled(act, NG, body)
                put_hi(NG - 1, TG - 2)
                put_hi(NG - 1, TG - 1)

            @block.vector
            def _(dve):
                pad = slice(4 * HD, P)
                nc.vector.memset(g.QT[pad, :, :].bitcast(F32), 0.0).then_inc(dve_pad, 1)
                nc.vector.memset(g.KT[pad, :, :].bitcast(F32), 0.0).then_inc(dve_pad, 1)
                dve.wait_ge(dve_pad, 2)
                nc.vector.memset(g.KT[4 * HD:ROWS, :, :].bitcast(F32), 1.0).then_inc(dve_pad, 1)
                for i in range(4):
                    n = NT // 4
                    dve.wait_ge(x_in[i], 16)
                    for t in range(i * n, (i + 1) * n):
                        nc.vector.bn_stats(stats[:, t, :], X[:, t, :]).then_inc(dve_step, 1)
                for t in range(NT):
                    if t == 0:
                        dve.wait_ge(dve_step, NT)
                    nc.vector.bn_aggr(mv[:, t, :], stats[:, t, :]).then_inc(dve_step, 1)
                dve.wait_ge(dve_step, 2 * NT)
                nc.vector.tensor_scalar(mv[:, :, 1], mv[:, :, 1], LN_EPS, None, ALU.add).then_inc(var_ready, 1)
                step = Chain(dve, passed, dve_step, 2 * NT)
                dve.wait_ge(tab_in, 64)
                step(nc.vector.tensor_scalar(nw[:, 0, :], nw_raw[:, 0, :], HD ** -0.5, None, ALU.mult))
                step(nc.vector.tensor_copy(nw[:, 1, :], nw_raw[:, 1, :]))
                half = HD // 2
                for qk in range(2):
                    for a in range(2):
                        own = nw[:, qk, a * half:(a + 1) * half].unsqueeze(1).to_broadcast([P, TPB, half])
                        other = nw[:, qk, (1 - a) * half:(2 - a) * half].unsqueeze(1).to_broadcast([P, TPB, half])
                        dst = slice(a * half, (a + 1) * half)
                        step(nc.vector.tensor_tensor(T1[:, :, qk, dst], C[:], own, ALU.mult))
                        step(nc.vector.scalar_tensor_tensor(out=T2[:, :, qk, dst], in0=S[:],
                                                            scalar=1.0 if a else -1.0, in1=other,
                                                            op0=ALU.mult, op1=ALU.mult))
                dve.wait_ge(std_ready, 1)
                step(nc.vector.reciprocal(rstd[:], std[:]))

                nc.vector.scalar_tensor_tensor(out=nmr[:], in0=mv[:, :, 0], scalar=-1.0, in1=rstd[:],
                                               op0=ALU.mult, op1=ALU.mult).then_inc(norm_ready, 1)
                step(nc.vector.tensor_reduce(w_max[:], nw[:], AX.X, ALU.max, apply_absolute_value=True))
                step(nc.vector.tensor_tensor(w_prod[:], w_max[:, 0:1], w_max[:, 1:2], ALU.mult))
                step(nc.vector.tensor_scalar(g.qk_small[:], w_prod[:], MAX_SCORE / HD, None, ALU.is_le))
                step(nc.vector.tensor_scalar(w_prod[:], w_prod[:], float(HD), None, ALU.mult))
                dve.wait_ge(zeros_ready, 1)
                nc.vector.tensor_scalar(shift[:], shift[:], w_prod[0:B * H, 0:1], None,
                                        ALU.subtract).then_inc(shift_ready, 1)

                def put_lo(it, j):
                    s, h = j % 2, j // 2
                    dve.wait_ge(hi_ready, at(it, TG, j + 1))
                    dve.wait_ge(parts_out[h], at(it, 64, 64))
                    nc.vector.tensor_tensor(lo[:, h, :, (j % 2) * P:(j % 2 + 1) * P], p_tq[s][:],
                                            hi[:, h, :, (j % 2) * P:(j % 2 + 1) * P].bitcast(F32),
                                            ALU.subtract).then_inc(lo_ready, 1)

                def body(it, first, last):
                    for j in range(TG):
                        s = j % 2
                        pos = (it % (NG // B)) * TG + j
                        dve.wait_ge(sq_ready, at(it, TG, j + 1))
                        wait(dve, rms_ready, at(it, TG, j - 1))
                        nc.vector.tensor_reduce(ms[:, s, :], sq[:, s, :].rearrange("p (g d) -> p g d", d=HD),
                                                AX.X, ALU.add).then_inc(reduced, 1)
                        dve.wait_ge(reduced, at(it, TG, j + 1))
                        nc.vector.tensor_scalar(ms[:, s, :], ms[:, s, :], 1.0 / HD, RMS_EPS,
                                                ALU.mult, ALU.add).then_inc(ms_ready, 1)
                        wait(dve, rc_ready, at(it, TG, j - 1))
                        dve.wait_ge(sq_ready, at(it, TG, j + 1))
                        qk4 = p_qk[s][:].rearrange("p (k h d) -> p k h d", k=2, d=HD)
                        ra4 = ra[:, s, :].rearrange("p (k h d) -> p k h d", k=2, d=HD)
                        rb4 = rb[:, s, :].rearrange("p (k h d) -> p k h d", k=2, d=HD)
                        nc.vector.tensor_tensor(ra4, qk4, T1[:, pos].unsqueeze(2).to_broadcast([P, 2, H, HD]),
                                                ALU.mult)
                        for a in range(2):
                            ins = nc.vector.tensor_tensor(
                                rb4[:, :, :, a * half:(a + 1) * half], qk4[:, :, :, (1 - a) * half:(2 - a) * half],
                                T2[:, pos, :, a * half:(a + 1) * half].unsqueeze(2).to_broadcast([P, 2, H, half]),
                                ALU.mult)
                        ins.then_inc(rb_ready, 1)
                        dve.wait_ge(rms_ready, at(it, TG, j + 1))
                        wait(dve, rd_ready, at(it, TG, j - 1))
                        nc.vector.reciprocal(ri[:, s, :], rms[:, s, :]).then_inc(ri_ready, 1)
                        if not (first and j < 2):
                            put_lo(*ahead(it, j - 2))
                peeled(dve, NG, body)
                put_lo(NG - 1, TG - 2)
                put_lo(NG - 1, TG - 1)

            @block.tensor
            def _(pe):
                pe.wait_ge(ident_ready, 2)

                def turn_x(it, j):
                    s = j % 2
                    pe.wait_ge(xn_ready, at(it, TG, j + 1))
                    wait(pe, xnT_ready, at(it, TG, j - 1))
                    for c in range(DC):
                        ins = pe.transpose(p_tp[s][:, c, :], xn[:, s, c * P:(c + 1) * P], ident[:])
                    ins.then_inc(xt_ready, 1)

                def turn_qk(it, j):
                    s = j % 2
                    pe.wait_ge(rd_ready, at(it, TG, j + 1))
                    wait(pe, lo_ready, at(it, TG, j - 1))
                    for c in range(4):
                        ins = pe.transpose(p_tq[s][:, c, :], rd[:, s, c * P:(c + 1) * P], ident[:])
                    ins.then_inc(tq_ready, 1)

                def body(it, first, last):
                    for j in range(TG):
                        s = j % 2
                        if not (last and j == TG - 1):
                            turn_x(*ahead(it, j + 1))
                        pe.wait_ge(xnT_ready, at(it, TG, j + 1))
                        wait(pe, rb_ready, at(it, TG, j - 1))
                        for c in range(DC):
                            pe.matmul(p_qk[s][:], xnT[:, s, c, :], W[:, c, 0:2 * D], start=(c == 0),
                                      stop=(c == DC - 1))
                        wait(pe, v_ready, at(it, TG, j - 1))
                        for c in range(DC):
                            ins = pe.matmul(p_v[s][:], xnT[:, s, c, :], W[:, c, 2 * D:3 * D], start=(c == 0),
                                            stop=(c == DC - 1))
                        ins.then_inc(qkv_ready, 1)
                        if not (first and j < 2):
                            turn_qk(*ahead(it, j - 2))
                turn_x(0, 0)
                pe.wait_ge(w_in, 48)
                peeled(pe, NG, body)
                turn_qk(NG - 1, TG - 2)
                turn_qk(NG - 1, TG - 1)


def load_quad_piece(sp, qk_parts, QT, KT, u, piece, landed):
    b, quad = u // (H // QH), u % (H // QH)
    for side, rows in ((0, (0, 0, 1, 1)), (1, (0, 1, 0, 1))):
        for r, part in enumerate(rows):
            src = qk_parts[part, side, b].rearrange("(q h d) t -> q d h t", h=QH, d=HD)[
                quad, :, :, piece * QW:(piece + 1) * QW]
            dst = (QT, KT)[side][r * HD:(r + 1) * HD, :, piece * QW:(piece + 1) * QW].bitcast(F32)
            sp.dma_start(dst, src).then_inc(landed, 16)


def load_shift(sp, neg_max, QT, u, piece, landed):
    src = neg_max.rearrange("(u o h) t -> u o h t", h=QH, o=1)[u, :, :, piece * QW:(piece + 1) * QW]
    sp.dma_start(QT[4 * HD:ROWS, :, piece * QW:(piece + 1) * QW].bitcast(F32), src).then_inc(landed, 16)


def rowmax(nc, g, s_, qk_parts, neg_max):
    QT, KT, ident, passed = g.QT, g.KT, g.ident, g.passed
    with ExitStack() as ctx:
        def sem(name):
            return ctx.enter_context(nc.semaphore(name))

        ident_r = s_("ident_r", [P, P], F32R)
        future_f = s_("future_f", [P, P])
        future = s_("future", [P, P], F32R)
        mx = s_("mx", [P, QH * TPB])
        neg = s_("neg", [QH * TPB, P], F32R)
        p_s = [ctx.enter_context(nc.psum_tensor(f"p_s{i}", [P, T], F32)) for i in range(2)]
        loaded = sem("loaded")
        consts = sem("consts")
        consts_r = sem("consts_r")
        rows_ready = sem("rows_ready")
        rows_read = sem("rows_read")
        mx_ready = sem("mx_ready")
        turned = sem("turned")
        neg_ready = sem("neg_ready")
        neg_out = sem("neg_out")
        NR = QH * TPB
        NLOAD = 8 * NQT * 16

        def unbounded(eng):
            return eng.If(eng.value_load(g.qk_small[0:1, 0:1], min_val=0, max_val=1) == 0)

        with nc.Block() as block:
            @block.sync
            def _(sp):
                with unbounded(sp):
                    for piece in range(NQT):
                        load_quad_piece(sp, qk_parts, QT, KT, 0, piece, loaded)
                    with sp.Fori(0, NU) as u:
                        wait_apart(sp, passed, turned, u + 1)
                        for piece in range(NQT):
                            load_quad_piece(sp, qk_parts, QT, KT, (u + 1) % NU, piece, loaded)
                        wait_apart(sp, passed, neg_ready, u + 1)
                        sp.dma_start(neg_max.rearrange("(u h) (t p) -> u (h t) p", h=QH, p=P)[u],
                                     neg[:].bitcast(F32)).then_inc(neg_out, 16)
                    sp.wait_ge(neg_out, NU * 16)
                    sp.wait_ge(loaded, (NU + 1) * NLOAD)

            @block.gpsimd
            def _(pool):
                with unbounded(pool):
                    pool.memset(future_f[:], 0.0).then_inc(consts, 1)
                    pool.wait_ge(consts, 1)
                    pool.affine_select(out=future_f[:], in_=future_f[:], compare_op=ALU.is_ge, fill=MASKED, base=0,
                                       pattern=[[-1, P]], channel_multiplier=1).then_inc(consts, 1)

            @block.tensor
            def _(pe):
                with unbounded(pe):
                    pe.wait_ge(consts_r, 2)
                    with pe.Fori(0, NU) as u:
                        pe.wait_ge(loaded, at(u, NLOAD, NLOAD))
                        for n in range(NR):
                            h, qb = n // TPB, n % TPB
                            buf = p_s[n % 2]
                            pe.wait_ge(mx_ready, at(u, NR, n + 1))
                            keys = (qb + 1) * P
                            q = QT[0:4 * HD, h, qb * P:(qb + 1) * P]
                            for k0 in range(0, keys - P, QW):
                                k1 = min(k0 + QW, keys - P)
                                pe.matmul(buf[:, k0:k1], q, KT[0:4 * HD, h, k0:k1], start=True, stop=True)
                            pe.matmul(buf[:, keys - P:keys], q, KT[0:4 * HD, h, keys - P:keys], start=True, stop=False)
                            pe.matmul(buf[:, keys - P:keys], ident_r[:], future[:], start=False,
                                      stop=True).then_inc(rows_ready, 1)
                        wait_apart(pe, passed, mx_ready, at(u, NR, NR + 2))
                        pe.transpose(p_s[0][0:NR, 0:P], mx[:], ident[:]).then_inc(turned, 1)
                        pe.wait_ge(neg_ready, u + 1)

            @block.vector
            def _(dve):
                with unbounded(dve):
                    dve.wait_ge(consts, 2)
                    nc.vector.tensor_copy(future[:], future_f[:]).then_inc(consts_r, 1)
                    nc.vector.tensor_copy(ident_r[:], ident[:]).then_inc(consts_r, 1)
                    dve.nop().then_inc(mx_ready, 2)
                    with dve.Fori(0, NU) as u:
                        for n in range(NR):
                            keys = (n % TPB + 1) * P
                            dve.wait_ge(rows_ready, at(u, NR, n + 1))
                            nc.vector.tensor_reduce(mx[:, n:n + 1], p_s[n % 2][:, 0:keys], AX.X,
                                                    ALU.max).then_inc(mx_ready, 1)
                        dve.wait_ge(turned, u + 1)
                        nc.vector.tensor_scalar(neg[:], p_s[0][0:NR, 0:P], -1.0, None, ALU.mult).then_inc(neg_ready, 1)
                        dve.wait_ge(neg_out, at(u, 16, 16))


def attention(nc, g, s_, wffn, qk_parts, neg_max, attn_t):
    QT, KT, V, vres, kq_in, passed = g.QT, g.KT, g.V, g.vres, g.kq_in, g.passed
    with ExitStack() as ctx:
        def sem(name):
            return ctx.enter_context(nc.semaphore(name))

        probs = [s_(f"probs{i}", [P, 3 * QW]) for i in range(NPB)]
        o_sb = [s_(f"o_sb{i}", [P, QW]) for i in range(2)]
        den = s_("den", [P, QW])
        rden = s_("rden", [P, QW])
        staged = s_("staged", [P, W_CHUNK])
        o_norm = [s_(f"o_norm{i}", [P, QW]) for i in range(2)]
        p_s = [ctx.enter_context(nc.psum_tensor(f"p_sc{i}", [P, 3 * QW], F32)) for i in range(2)]
        p_o = [ctx.enter_context(nc.psum_tensor(f"p_o{i}", [P, QW], F32)) for i in range(2)]

        w_in = sem("w_staged")
        w_step = sem("w_step")
        v_in = sem("v_in")
        scores_ready = sem("scores_ready")
        probs_ready = sem("probs_ready")
        masked = sem("masked")
        probs_used = sem("probs_used")
        o_copied = sem("o_copied")
        den_ready = sem("den_ready")
        rden_ready = sem("rden_ready")
        o_ready = sem("o_ready")
        o_out = [sem(f"o_out{i}") for i in range(2)]
        NDMA = 9 * 16

        with nc.Block() as block:
            @block.sync
            def _(sp):
                for s in range(2):
                    sp.nop().then_inc(o_out[s], 64)
                for piece in reversed(range(NQT)):
                    load_shift(sp, neg_max, QT, 0, piece, kq_in[piece])
                sp.dma_start(staged[:], wffn[0]).then_inc(w_in, 16)

                def body(u, last):
                    b, quad = u // (H // QH), u % (H // QH)
                    for i, piece in enumerate(reversed(range(NQT))):
                        if not last:
                            wait_apart(sp, passed, scores_ready, at(u, NGR, LAST[piece] + 1))
                            load_quad_piece(sp, qk_parts, QT, KT, u + 1, piece, kq_in[piece])
                            load_shift(sp, neg_max, QT, u + 1, piece, kq_in[piece])
                        if i == 1 and not last:
                            wait_apart(sp, passed, w_step, at(u, 3, 3))
                            sp.dma_start(staged[:], wffn[u + 1]).then_inc(w_in, 16)
                        wait_apart(sp, passed, o_ready, at(u, NQT, i + 1))
                        for h in range(QH):
                            sp.dma_start(attn_t[b].rearrange("(q h d) t -> q h d t", h=QH, d=HD)[
                                quad, h, :, piece * QW:(piece + 1) * QW],
                                o_norm[i % 2][h * STRIP:h * STRIP + HD, :]).then_inc(o_out[i % 2], 16)
                with sp.Fori(0, NU - 1) as u:
                    body(u, False)
                body(NU - 1, True)
                for s in range(2):
                    sp.wait_ge(o_out[s], (NU * NQT // 2 + 1) * 64)

            @block.gpsimd
            def _(pool):
                def put_v(u, piece):
                    nc.gpsimd.tensor_copy(V[:, piece * KPQ:(piece + 1) * KPQ, :, 0:HD],
                                          vres[:, u, piece * KPQ:(piece + 1) * KPQ, :].rearrange(
                                              "p k (h d) -> p k h d", d=HD)).then_inc(v_in, 1)

                for piece in reversed(range(NQT)):
                    put_v(0, piece)

                def mask(buf, kinds):
                    b0 = 0
                    while b0 < len(kinds):
                        tri, m = kinds[b0], b0 + 1
                        if len(tri) == 1:
                            while m < len(kinds) and kinds[m] == tri:
                                m += 1
                            v = buf[:, b0 * QW:m * QW].rearrange("p (n c) -> p n c", c=QW)[:, :, 0:P]
                        elif tri:
                            v = buf[:, b0 * QW:m * QW].rearrange("p (a c) -> p a c", c=P)[
                                :, 0:tri[1] // P + 1:tri[1] // P, :]
                        if tri:
                            ins = nc.gpsimd.affine_select(out=v, in_=v, compare_op=ALU.is_ge, fill=0.0, base=0,
                                                          pattern=[[0, v.shape[1]], [1, P]],
                                                          channel_multiplier=-1)
                        b0 = m
                    return ins

                def body(u, last):
                    n = 0
                    for i, (qt, banks, ends) in enumerate(GROUPS):
                        if HAS_TRI[i]:
                            n += 1
                            wait_apart(pool, passed, probs_ready, at(u, NGR, i + 1 + 2))
                            mask(probs[i % NPB], [tuple(tri) for _, tri in banks]).then_inc(masked, 1)
                            if not HAS_TRI[(i + 1) % NGR] or GROUPS[(i + 1) % NGR][0] != qt:
                                if not last and qt < NQT - 1:
                                    pool.wait_ge(probs_used, at(u, NGR, LAST[qt + 1] + 1 + NPB))
                                    put_v(u + 1, qt + 1)
                    if not last:
                        pool.wait_ge(probs_used, at(u, NGR, LAST[0] + 1 + NPB))
                        put_v(u + 1, 0)
                with pool.Fori(0, NU - 1) as u:
                    body(u, False)
                body(NU - 1, True)

            @block.scalar
            def _(act):
                act.nop().then_inc(probs_ready, 2)
                with act.Fori(0, NU) as u:
                    for i, (qt, banks, ends) in enumerate(GROUPS):
                        n = len(banks) * QW
                        act.wait_ge(scores_ready, at(u, NGR, i + 1))
                        act.wait_ge(probs_used, at(u, NGR, i + 1))
                        nc.scalar.activation(probs[i % NPB][:, 0:n], p_s[i % 2][:, 0:n],
                                             ACT.Exp).then_inc(probs_ready, 1)

            @block.tensor
            def _(pe):
                pe.nop().then_inc(probs_used, NPB)

                def scores(u, i):
                    qt, banks, _ = GROUPS[i]
                    for piece in range(NQT):
                        if i == FIRST[piece]:
                            pe.wait_ge(kq_in[piece], at(u, NDMA, NDMA))
                    pe.wait_ge(probs_ready, at(u, NGR, i + 1))
                    for n, (items, _) in enumerate(banks):
                        for kb, h, q0, w, c in items:
                            ins = pe.matmul(p_s[i % 2][:, n * QW + c:n * QW + c + w],
                                            KT[:, h, kb * P:(kb + 1) * P],
                                            QT[:, h, qt * QW + q0:qt * QW + q0 + w],
                                            start=True, stop=True)
                    ins.then_inc(scores_ready, 1)

                def values(u, i):
                    qt, banks, ends = GROUPS[i]
                    order = NQT - 1 - qt
                    if i == 0 or GROUPS[i - 1][0] != qt:
                        pe.wait_ge(o_copied, at(u, NQT, order + 1))
                    if qt == NQT - 1:
                        piece = min(kb for items, _ in banks for kb, *_ in items) // KPQ
                        pe.wait_ge(v_in, at(u, NQT, NQT - piece))
                    pe.wait_ge(probs_ready, at(u, NGR, i + 1 + 2))
                    if HAS_TRI[i]:
                        pe.wait_ge(masked, at(u, NMASK, sum(HAS_TRI[:i + 1])))
                    for n, (items, _) in enumerate(banks):
                        for kb, h, q0, w, c in items:
                            ins = pe.matmul(p_o[order % 2][h * STRIP:(h + 1) * STRIP, q0:q0 + w],
                                            V[:, kb, h, :], probs[i % NPB][:, n * QW + c:n * QW + c + w],
                                            start=(kb == KPQ * qt), stop=(kb == (0 if qt else 3)),
                                            skip_group_check=True)
                    ins.then_inc(probs_used, 1)

                def body(u, first, last):
                    for i in range(NGR):
                        if i + 2 < NGR:
                            scores(u, i + 2)
                        elif not last:
                            scores(u + 1, i + 2 - NGR)
                        if i >= 1:
                            values(u, i - 1)
                        elif not first:
                            values(u - 1, NGR - 1)
                scores(0, 0)
                scores(0, 1)
                peeled(pe, NU, body)
                values(NU - 1, NGR - 1)

            @block.vector
            def _(dve):
                dve.nop().then_inc(o_copied, 2)

                def round_weights(u):
                    dve.wait_ge(w_in, at(u, 16, 16))
                    nc.vector.tensor_copy(g.Wr[:, u, :], staged[:]).then_inc(w_step, 1)
                    dve.wait_ge(w_step, at(u, 3, 1))
                    nc.vector.tensor_tensor(staged[:], staged[:], g.Wr[:, u, :].bitcast(F32),
                                            ALU.subtract).then_inc(w_step, 1)
                    dve.wait_ge(w_step, at(u, 3, 2))
                    nc.vector.tensor_reduce(g.w_diff[:, bass.ds(u, 1)], staged[:], AX.X, ALU.max,
                                            apply_absolute_value=True).then_inc(w_step, 1)
                with dve.Fori(0, NU) as u:
                    for i, qt in enumerate(reversed(range(NQT))):
                        dve.wait_ge(probs_used, at(u, NGR, LAST[qt] + 1 + NPB))
                        nc.vector.tensor_copy(o_sb[i % 2][:], p_o[i % 2][:]).then_inc(o_copied, 1)
                        wait_apart(dve, passed, o_copied, at(u, NQT, i + 1 + 2))
                        nc.vector.stream_shuffle(den[:], o_sb[i % 2][:], [HD] * STRIP).then_inc(den_ready, 1)
                        dve.wait_ge(den_ready, at(u, NQT, i + 1))
                        nc.vector.reciprocal(rden[:], den[:]).then_inc(rden_ready, 1)
                        dve.wait_ge(rden_ready, at(u, NQT, i + 1))
                        dve.wait_ge(o_out[i % 2], at(u, 128, 64 * (i // 2) + 64))
                        nc.vector.tensor_tensor(o_norm[i % 2][:], o_sb[i % 2][:], rden[:], ALU.mult).then_inc(o_ready, 1)
                        if i == 0:
                            round_weights(u)


def mix(nc, g, s_, x, wo, wffn, attn_t, x2_s, xf_t):
    ident, passed = g.ident, g.passed
    N_LATE = W_CHUNKS - W_KEPT
    with ExitStack() as ctx:
        def sem(name):
            return ctx.enter_context(nc.semaphore(name))

        Wo = s_("Wo", [P, DC, D])
        X = s_("X_again", [P, NT, D])
        staged = s_("staged_late", [P, N_LATE, W_CHUNK])
        ones = s_("ones", [P, 1])
        worst = s_("worst", [P, 1])
        at_in = s_("at_in", [P, DC, QW])
        st = s_("st", [P, 2, TG, 6])
        mv = s_("mv2", [P, 2, TG, 2])
        sd = s_("sd", [P, 2, TG])
        rs = s_("rs", [P, 2, TG])
        t1 = s_("t1", [P, TG, D])
        x2 = s_("x2", [P, TG, D])
        xf = s_("xf", [P, TG, D])
        xfT = s_("xfT", [P, DC, QW])
        p_y = [ctx.enter_context(nc.psum_tensor(f"p_y{j}", [P, D], F32)) for j in range(TG)]
        p_x = [ctx.enter_context(nc.psum_tensor(f"p_x{j}", [P, DC, P], F32)) for j in range(TG)]
        wo_in = sem("wo_in")
        x_in = sem("x_again_in")
        w_in = sem("w_late_in")
        rounded = sem("rounded")
        diff_ready = sem("diff_ready")
        diff_read = sem("diff_read")
        ones_ready = sem("ones_m")
        worst_step = sem("worst_step")
        summed = sem("summed")
        attn_in = sem("attn_in")
        y_ready = sem("y_ready")
        step_m = sem("step_m")
        var_ready = sem("var_m")
        std_ready = sem("std_m")
        xf_ready = sem("xf_ready")
        xt_ready = sem("xt_m")
        xfT_ready = sem("xfT_ready")
        stored = sem("stored")
        X2_STEP = TG + TG + 1 + TG + TG
        NCH = X2_STEP + TG + TG + 1

        with nc.Block() as block:
            @block.sync
            def _(sp):
                sp.nop().then_inc(stored, 32)
                sp.dma_start(Wo[:], wo.rearrange("(c p) n -> p c n", p=P)).then_inc(wo_in, 16)

                def load(turn):
                    sp.dma_start(at_in[:], attn_t[turn // (NG // B)].rearrange("(c p) t -> p c t", p=P)[
                        :, :, bass.ds((turn % (NG // B)) * QW, QW)]).then_inc(attn_in, 16)
                load(0)
                sp.dma_start(X[:], x.rearrange("(t p) d -> p t d", p=P)).then_inc(x_in, 16)
                for i in range(N_LATE):
                    sp.dma_start(staged[:, i, :], wffn[W_KEPT + i]).then_inc(w_in, 16)
                with sp.Fori(0, NG) as it:
                    wait_apart(sp, passed, y_ready, at(it, TG, TG))
                    load((it + 1) % NG)
                    wait_apart(sp, passed, step_m, at(it, NCH, X2_STEP))
                    sp.dma_start(x2_s.rearrange("(g t) p d -> g p t d", t=TG)[it], x2[:]).then_inc(stored, 16)
                    wait_apart(sp, passed, xfT_ready, at(it, TG, TG))
                    sp.dma_start(xf_t.rearrange("(c p) t -> p c t", p=P)[:, :, bass.ds(it * QW, QW)],
                                 xfT[:]).then_inc(stored, 16)
                sp.wait_ge(stored, (NG + 1) * 32)
                sp.wait_ge(attn_in, (NG + 1) * 16)

            @block.tensor
            def _(pe):
                pe.wait_ge(wo_in, 16)
                with pe.Fori(0, NG) as it:
                    pe.wait_ge(attn_in, at(it, 16, 16))
                    for j in range(TG):
                        for c in range(DC):
                            ins = pe.matmul(p_y[j][:], at_in[:, c, j * P:(j + 1) * P], Wo[:, c, :],
                                            start=(c == 0), stop=(c == DC - 1))
                        ins.then_inc(y_ready, 1)
                    pe.wait_ge(xf_ready, it + 1)
                    for j in range(TG):
                        for c in range(DC):
                            ins = pe.transpose(p_x[j][:, c, :], xf[:, j, c * P:(c + 1) * P], ident[:])
                        ins.then_inc(xt_ready, 1)

                pe.wait_ge(worst_step, 1)
                pe.wait_ge(ones_ready, 1)
                pe.matmul(p_y[0][0:1, 0:1], worst[:], ones[:], start=True, stop=True).then_inc(summed, 1)

            @block.gpsimd
            def _(pool):
                pool.memset(ones[:], 1.0).then_inc(ones_ready, 1)
                for i in range(N_LATE):
                    pool.wait_ge(rounded, i + 1)
                    nc.gpsimd.tensor_tensor(staged[:, i, :], staged[:, i, :], g.Wr[:, W_KEPT + i, :].bitcast(F32),
                                            ALU.subtract).then_inc(diff_ready, 1)

            @block.scalar
            def _(act):
                act.wait_ge(w_in, N_LATE * 16)
                for i in range(N_LATE):
                    nc.scalar.copy(g.Wr[:, W_KEPT + i, :], staged[:, i, :]).then_inc(rounded, 1)
                with act.Fori(0, NG) as it:
                    for k in range(2):
                        act.wait_ge(var_ready, at(it, 2, k + 1))
                        nc.scalar.activation(sd[:, k], mv[:, k, :, 1], ACT.Sqrt).then_inc(std_ready, 1)
                    act.wait_ge(stored, at(it, 32, 32))
                    for j in range(TG):
                        act.wait_ge(xt_ready, at(it, TG, j + 1))
                        nc.scalar.copy(xfT[:, :, j * P:(j + 1) * P], p_x[j][:]).then_inc(xfT_ready, 1)

            @block.vector
            def _(dve):
                dve.wait_ge(x_in, 16)
                with dve.Fori(0, NG) as it:
                    step = Chain(dve, passed, step_m, at(it, NCH, 0))
                    for j in range(TG):
                        dve.wait_ge(y_ready, at(it, TG, j + 1))
                        step(nc.vector.bn_stats(st[:, 0, j], p_y[j][:]))
                    for j in range(TG):
                        step(nc.vector.bn_aggr(mv[:, 0, j], st[:, 0, j]))
                    nc.vector.tensor_scalar(mv[:, 0, :, 1], mv[:, 0, :, 1], LN_EPS, None,
                                            ALU.add).then_inc(var_ready, 1)
                    dve.wait_ge(std_ready, at(it, 2, 1))
                    step(nc.vector.reciprocal(rs[:, 0], sd[:, 0]))
                    for j in range(TG):
                        step(nc.vector.tensor_scalar(t1[:, j], p_y[j][:], mv[:, 0, j, 0:1], rs[:, 0, j:j + 1],
                                                     ALU.subtract, ALU.mult))
                    dve.wait_ge(stored, at(it, 32, 32))
                    for j in range(TG):
                        step(nc.vector.tensor_tensor(x2[:, j], t1[:, j], X[:, it * TG + j], ALU.add))
                    assert step.n == X2_STEP
                    for j in range(TG):
                        step(nc.vector.bn_stats(st[:, 1, j], x2[:, j]))
                    for j in range(TG):
                        step(nc.vector.bn_aggr(mv[:, 1, j], st[:, 1, j]))
                    nc.vector.tensor_scalar(mv[:, 1, :, 1], mv[:, 1, :, 1], LN_EPS, None,
                                            ALU.add).then_inc(var_ready, 1)
                    dve.wait_ge(std_ready, at(it, 2, 2))
                    step(nc.vector.reciprocal(rs[:, 1], sd[:, 1]))
                    assert step.n == NCH
                    for j in range(TG):
                        ins = nc.vector.tensor_scalar(xf[:, j], x2[:, j], mv[:, 1, j, 0:1], rs[:, 1, j:j + 1],
                                                      ALU.subtract, ALU.mult)
                    ins.then_inc(xf_ready, 1)
                for i in range(N_LATE):
                    dve.wait_ge(diff_ready, i + 1)
                    nc.vector.tensor_reduce(g.w_diff[:, W_KEPT + i:W_KEPT + i + 1], staged[:, i, :], AX.X, ALU.max,
                                            apply_absolute_value=True).then_inc(diff_read, 1)
                dve.wait_ge(diff_read, N_LATE)
                nc.vector.tensor_reduce(worst[:], g.w_diff[:], AX.X, ALU.max).then_inc(worst_step, 1)
                dve.wait_ge(summed, 1)
                nc.vector.tensor_scalar(g.w_exact[0:1, :], p_y[0][0:1, 0:1], 0.0, None, ALU.is_le)


def ffn(nc, g, s_, wffn, w1s, w2s, h1s, h2s, w3s, x2_s, xf_t, out):
    passed = g.passed
    with ExitStack() as ctx:
        def sem(name):
            return ctx.enter_context(nc.semaphore(name))

        S = s_("Sc", [P, 4, HC])
        S3 = s_("S3", [P, D])
        xfT = s_("xfT_in", [P, DC, QW])
        x2 = s_("x2_in", [P, TG, D])
        gate = [s_(f"gate{i}", [P, QW]) for i in range(2)]
        y = s_("y", [P, TG, D])
        st = s_("st3", [P, TG, 6])
        mv = s_("mv3", [P, TG, 2])
        sd = s_("sd3", [P, TG])
        rs = s_("rs3", [P, TG])
        o1 = s_("o1", [P, TG, D])
        ob = s_("ob", [P, TG, D])
        xs = s_("xs", [P, 2, DC, QW], F32R)
        NT_ = 3
        temp = [s_(f"temp{i}", [P, QW]) for i in range(NT_)]
        split_at = s_.at
        ha_s = s_("ha_s", [P, 2, HC, QW], F32R)
        hb_s = s_("hb_s", [P, 2, HC, QW], F32R)
        whole = Arena(nc, split_at)
        ha = whole("ha", [P, HC, QW])
        hb = whole("hb", [P, HC, QW])
        NBK = 6
        USES = 2 * HC + HC + HC + TG
        CHUNKS = 3 * HC
        assert USES % NBK == 0 and CHUNKS % NT_ == 0
        bank = [ctx.enter_context(nc.psum_tensor(f"bank{i}", [P, QW], F32)) for i in range(NBK)]
        s_in = sem("s_in")
        w_in = [sem(f"w_in{i}") for i in range(4)]
        xf_in = sem("xf_in")
        x2_in = sem("x2_in_s")
        pe_ready = sem("pe_ready")
        gate_ready = sem("gate_ready")
        h1_ready = sem("h1_ready")
        h23_ready = sem("h23_ready")
        xs_ready = sem("xs_ready")
        parts_ready = sem("parts_ready")
        y_ready = sem("y3_ready")
        step_f = sem("step_f")
        var_ready = sem("var_f")
        std_ready = sem("std_f")
        ob_ready = sem("ob_ready")
        out_done = sem("out_done")
        NCH = TG + TG + 1 + TG
        NPARTS = 2 * CHUNKS
        ov = out.rearrange("(g t p) d -> g p t d", t=TG, p=P)

        def weights(Wx):
            flat = Wx[:].rearrange("p q e -> p (q e)")
            cut, mats = 0, []
            for rows, cols in ((D, HID), (D, HID), (HID, D), (HID, HID), (HID, HID)):
                size = rows // P * cols
                mats.append(flat[:, cut:cut + size].rearrange("p (c n) -> p c n", n=cols))
                cut += size
            return mats

        def by_weights(eng, program):
            exact = eng.value_load(g.w_exact[0:1, 0:1], min_val=0, max_val=1)
            with eng.If(exact == 1):
                program(True)
            with eng.If(exact == 0):
                program(False)

        with nc.Block() as block:
            @block.sync
            def _(sp):
                sp.nop().then_inc(out_done, 16)
                for i, w in enumerate((w1s, w2s, h1s, h2s)):
                    sp.dma_start(S[:, i, :], w).then_inc(s_in, 16)
                sp.dma_start(S3[:], w3s.partition_broadcast(P)).then_inc(s_in, 16)

                def load_xf(turn):
                    sp.dma_start(xfT[:], xf_t.rearrange("(c p) t -> p c t", p=P)[:, :, bass.ds(turn * QW, QW)]
                                 ).then_inc(xf_in, 16)

                def load_x2(turn):
                    sp.dma_start(x2[:], x2_s.rearrange("(g t) p d -> g p t d", t=TG)[turn]).then_inc(x2_in, 16)
                load_xf(0)
                load_x2(0)
                with sp.If(sp.value_load(g.w_exact[0:1, 0:1], min_val=0, max_val=1) == 0):
                    for i in range(W_CHUNKS):
                        sp.dma_start(g.Wf[:, i, :], wffn[i]).then_inc(w_in[max(0, (i + 1) // 4)], 16)
                    for i in range(3):
                        sp.wait_ge(w_in[i], (3, 4, 4)[i] * 16)

                def store(turn):
                    sp.dma_start(ov[turn], ob[:]).then_inc(out_done, 16)

                def body(it, first):
                    wait_apart(sp, passed, pe_ready, at(it, USES, 2 * HC))
                    load_xf((it + 1) % NG)
                    if not first:
                        wait_apart(sp, passed, ob_ready, it)
                        store(it - 1)
                        load_x2(it)
                body(0, True)
                with sp.Fori(1, NG) as it:
                    body(it, False)
                sp.wait_ge(ob_ready, NG)
                store(NG - 1)
                sp.wait_ge(out_done, (NG + 1) * 16)
                sp.wait_ge(xf_in, (NG + 1) * 16)
                sp.wait_ge(x2_in, NG * 16)

            @block.tensor
            def _(pe):
                def wait_read(it, n):
                    turn, n = (0, n) if n >= 0 else (-1, n + USES)
                    if n >= 4 * HC:
                        pe.wait_ge(y_ready, at(it, TG, TG + TG * turn + n - 4 * HC + 1))
                    elif n >= 2 * HC:
                        pe.wait_ge(h23_ready, at(it, 2 * HC, 2 * HC + 2 * HC * turn + n - 2 * HC + 1))
                    elif n % 2:
                        pe.wait_ge(h1_ready, at(it, HC, 2 + n // 2 + 1))
                    else:
                        pe.wait_ge(gate_ready, at(it, HC, n // 2 + 1))

                def program(exact):
                    W1, W2, W3, H1, H2 = weights(g.Wr if exact else g.Wf)
                    order = [(p, c) for p in range(2) for c in range(HC - 1)] + [(0, HC - 1), (1, HC - 1)]
                    if not exact:
                        pe.wait_ge(w_in[0], 3 * 16)
                        pe.wait_ge(w_in[1], 4 * 16)
                        pe.wait_ge(w_in[2], 4 * 16)
                    with pe.Fori(0, NG) as it:
                        n = 0

                        def use(width, steps):
                            nonlocal n
                            b = n % NBK
                            wait_read(it, n - NBK)
                            for k, (w, m, part) in enumerate(steps):
                                if part is not None:
                                    pe.wait_ge(parts_ready, at(it, NPARTS, 2 * NT_ + part + 1))
                                ins = pe.matmul(bank[b][:, 0:width], w, m, start=(k == 0), stop=(k == len(steps) - 1))
                            ins.then_inc(pe_ready, 1)
                            n += 1

                        if exact:
                            pe.wait_ge(xs_ready, at(it, 2 * DC, 2 * DC))
                        else:
                            pe.wait_ge(xf_in, at(it, 16, 16))
                        for m in range(HC):
                            for W in (W1, W2):
                                col = slice(m * P, (m + 1) * P)
                                if exact:
                                    use(QW, [(W[:, c, col], xs[:, p, c, :], None) for p in range(2) for c in range(DC)])
                                else:
                                    use(QW, [(W[:, c, col], xfT[:, c, :], None) for c in range(DC)])
                        for layer, (W, src_s, src) in enumerate(((H1, ha_s, ha), (H2, hb_s, hb))):
                            if not exact:
                                pe.wait_ge(*((h1_ready, at(it, HC, HC + 2)),
                                             (h23_ready, at(it, 2 * HC, 3 * HC)))[layer])
                            for m in range(HC):
                                col = slice(m * P, (m + 1) * P)
                                if exact:
                                    use(QW, [(W[:, c, col], src_s[:, p, c, :],
                                              2 * (layer * HC + c) + p if m == 0 else None) for p, c in order])
                                else:
                                    use(QW, [(W[:, c, col], src[:, c, :], None) for c in range(HC)])
                        if not exact:
                            pe.wait_ge(h23_ready, at(it, 2 * HC, 4 * HC))
                        for j in range(TG):
                            tok = slice(j * P, (j + 1) * P)
                            if exact:
                                use(D, [(ha_s[:, p, c, tok], W3[:, c, :], 2 * (2 * HC + c) + p if j == 0 else None)
                                        for p, c in order])
                            else:
                                use(D, [(ha[:, c, tok], W3[:, c, :], None) for c in range(HC)])
                by_weights(pe, program)

            @block.scalar
            def _(act):
                act.nop().then_inc(h23_ready, 2 * HC)
                act.wait_ge(s_in, 5 * 16)

                def tail(turn):
                    act.wait_ge(var_ready, turn + 1)
                    nc.scalar.activation(sd[:], mv[:, :, 1], ACT.Sqrt).then_inc(std_ready, 1)

                def program(exact):
                    def body(it, first):
                        for m in range(HC):
                            n = 2 * m
                            act.wait_ge(pe_ready, at(it, USES, n + 1))
                            act.wait_ge(h1_ready, at(it, HC, m + 1))
                            nc.scalar.activation(gate[m % 2][:], bank[n % NBK][:], ACT.Silu,
                                                 scale=S[:, 0, m:m + 1]).then_inc(gate_ready, 1)
                        if not first:
                            tail(it - 1)
                        for layer, whole_out in ((2, hb), (3, ha)):
                            for m in range(HC):
                                n = layer * HC + m
                                k = (layer - 1) * HC + m
                                act.wait_ge(pe_ready, at(it, USES, n + 1))
                                if exact:
                                    act.wait_ge(parts_ready, at(it, NPARTS, 2 * k + 2))
                                dst = temp[k % NT_][:] if exact else whole_out[:, m, :]
                                nc.scalar.activation(dst, bank[n % NBK][:], ACT.Gelu,
                                                     scale=S[:, layer, m:m + 1]).then_inc(h23_ready, 1)
                    body(0, True)
                    with act.Fori(1, NG) as it:
                        body(it, False)
                    tail(NG - 1)
                by_weights(act, program)

            @block.vector
            def _(dve):
                dve.nop().then_inc(h1_ready, 2)
                dve.nop().then_inc(y_ready, TG)
                dve.nop().then_inc(parts_ready, 2 * NT_)
                dve.wait_ge(s_in, 5 * 16)

                def split_input(turn):
                    dve.wait_ge(xf_in, at(turn, 16, 16))
                    for c in range(DC):
                        nc.vector.tensor_copy(xs[:, 0, c], xfT[:, c]).then_inc(xs_ready, 1)
                        dve.wait_ge(xs_ready, at(turn, 2 * DC, 2 * c + 1))
                        nc.vector.tensor_tensor(xs[:, 1, c], xfT[:, c], xs[:, 0, c].bitcast(F32),
                                                ALU.subtract).then_inc(xs_ready, 1)

                def split(it, k, dst, m):
                    t = temp[k % NT_]
                    nc.vector.tensor_copy(dst[:, 0, m], t[:]).then_inc(parts_ready, 1)
                    dve.wait_ge(parts_ready, at(it, NPARTS, 2 * NT_ + 2 * k + 1))
                    nc.vector.tensor_tensor(dst[:, 1, m], t[:], dst[:, 0, m].bitcast(F32),
                                            ALU.subtract).then_inc(parts_ready, 1)

                def tail(turn):
                    step = Chain(dve, passed, step_f, at(turn, NCH, 0))
                    dve.wait_ge(y_ready, at(turn, TG, 2 * TG))
                    for j in range(TG):
                        step(nc.vector.bn_stats(st[:, j], y[:, j]))
                    for j in range(TG):
                        step(nc.vector.bn_aggr(mv[:, j], st[:, j]))
                    nc.vector.tensor_scalar(mv[:, :, 1], mv[:, :, 1], LN_EPS, None, ALU.add).then_inc(var_ready, 1)
                    dve.wait_ge(std_ready, turn + 1)
                    step(nc.vector.reciprocal(rs[:], sd[:]))
                    for j in range(TG):
                        step(nc.vector.tensor_scalar(o1[:, j], y[:, j], mv[:, j, 0:1], rs[:, j:j + 1],
                                                     ALU.subtract, ALU.mult))
                    dve.wait_ge(x2_in, at(turn, 16, 16))
                    dve.wait_ge(out_done, at(turn, 16, 16))
                    assert step.n == NCH
                    for j in range(TG):
                        ins = nc.vector.tensor_tensor(ob[:, j], o1[:, j], x2[:, j], ALU.add)
                    ins.then_inc(ob_ready, 1)

                def program(exact):
                    if exact:
                        split_input(0)

                    def body(it, first):
                        for m in range(HC):
                            n = 2 * m + 1
                            dve.wait_ge(pe_ready, at(it, USES, n + 1))
                            dve.wait_ge(gate_ready, at(it, HC, m + 1))
                            if exact:
                                dve.wait_ge(parts_ready, at(it, NPARTS, 2 * m + 2))
                            dst = temp[m % NT_][:] if exact else ha[:, m, :]
                            nc.vector.scalar_tensor_tensor(out=dst, in0=bank[n % NBK][:], scalar=S[:, 1, m:m + 1],
                                                           in1=gate[m % 2][:], op0=ALU.mult,
                                                           op1=ALU.mult).then_inc(h1_ready, 1)
                            if exact:
                                dve.wait_ge(h1_ready, at(it, HC, 2 + m + 1))
                                split(it, m, ha_s, m)
                        if not first:
                            tail(it - 1)
                        if exact:
                            for layer, dst in ((2, hb_s), (3, ha_s)):
                                for m in range(HC):
                                    dve.wait_ge(h23_ready, at(it, 2 * HC, 2 * HC + (layer - 2) * HC + m + 1))
                                    split(it, (layer - 1) * HC + m, dst, m)
                                if layer == 2:
                                    split_input(it + 1)
                        for j in range(TG):
                            n = 4 * HC + j
                            dve.wait_ge(pe_ready, at(it, USES, n + 1))
                            nc.vector.tensor_tensor(y[:, j], bank[n % NBK][:, 0:D], S3[:], ALU.mult).then_inc(y_ready, 1)
                    body(0, True)
                    with dve.Fori(1, NG) as it:
                        body(it, False)
                    tail(NG - 1)
                by_weights(dve, program)


def kernel(L0_attn_x, L0_attn_Wq, L0_attn_Wk, L0_attn_Wv, L0_attn_Wo, L0_attn_q_norm_w, L0_attn_k_norm_w,
           L0_ffn_w1_w, L0_ffn_w1_s, L0_ffn_w2_w, L0_ffn_w2_s, L0_ffn_h1_w, L0_ffn_h1_s, L0_ffn_h2_w,
           L0_ffn_h2_s, L0_ffn_w3_w, L0_ffn_w3_s):
    import concourse.bacc as bacc
    from concourse.bass_utils import run_bass_kernel_spmd

    def chunks(w):
        w = np.asarray(w).T
        w = w.reshape(-1, P, w.shape[1]).transpose(1, 0, 2).reshape(P, -1, W_CHUNK)
        return w.transpose(1, 0, 2)

    def columns(s):
        return np.ascontiguousarray(np.asarray(s).reshape(HC, P).T)

    inv_freq = (1.0 / np.float32(10000.0) ** (np.arange(0, HD, 2, dtype=np.float32) / np.float32(HD)))
    angle = np.outer(np.arange(T, dtype=np.float32), inv_freq.astype(np.float32)).astype(np.float32)
    arrays = {
        "x": np.ascontiguousarray(np.asarray(L0_attn_x).reshape(B * T, D)),
        "wq": np.asarray(L0_attn_Wq), "wk": np.asarray(L0_attn_Wk), "wv": np.asarray(L0_attn_Wv),
        "wo": np.asarray(L0_attn_Wo), "qw": np.asarray(L0_attn_q_norm_w), "kw": np.asarray(L0_attn_k_norm_w),
        "cos": np.cos(angle), "sin": np.sin(angle),
        "wffn": np.ascontiguousarray(np.concatenate(
            [chunks(w) for w in (L0_ffn_w1_w, L0_ffn_w2_w, L0_ffn_w3_w, L0_ffn_h1_w, L0_ffn_h2_w)])),
        "w1s": columns(L0_ffn_w1_s), "w2s": columns(L0_ffn_w2_s),
        "h1s": columns(L0_ffn_h1_s), "h2s": columns(L0_ffn_h2_s), "w3s": np.asarray(L0_ffn_w3_s),
    }
    nc = bacc.Bacc("TRN2", target_bir_lowering=False, num_devices=1)
    args = [nc.dram_tensor(n, a.shape, mybir.dt.from_np(a.dtype), kind="ExternalInput").ap()
            for n, a in arrays.items()]
    out = nc.dram_tensor("out", (B * T, D), F32, kind="ExternalOutput").ap()
    build(nc, *args, out)
    r = run_bass_kernel_spmd(nc, [arrays], core_ids=[0])
    return r.results[0]["out"].reshape(B, T, D)
```

```python
from contextlib import ExitStack

import numpy as np
import concourse.bass as bass
from concourse import mybir

F32 = mybir.dt.float32
F32R = mybir.dt.float32r
I32 = mybir.dt.int32
ALU = mybir.AluOpType
ACT = mybir.ActivationFunctionType
AX = mybir.AxisListType

P = 128
B, T, D = 2, 2048, 256
H, HD = 16, 16
HID = 1024
NT = B * T // P
TPB = T // P
DC = D // P
HC = HID // P
QH = 4
NU = B * H // QH
QW = 512
NQT = T // QW
KPQ = QW // P
ROWS = 4 * HD + 1
STRIP = 32
LN_EPS = 1e-5
RMS_EPS = 1e-6
MASKED = -1e30
TG = 4
NG = NT // TG
MAX_SCORE = 40.0
W_CHUNK = 2048
W_CHUNKS = (2 * D * HID + 2 * HID * HID + HID * D) // P // W_CHUNK
W_KEPT = 8
N_LATE = W_CHUNKS - W_KEPT


class Shared:
    pass


class Arena:

    def __init__(self, nc, start):
        self.nc, self.at = nc, start

    def __call__(self, name, shape, dt=F32):
        t = self.nc.alloc_sbuf_tensor_at(name, shape, dt, offset=self.at)
        self.at += -(-4 * int(np.prod(shape[1:])) // 32) * 32
        return t


def at(it, per, n):
    return it * per + n


def wait(eng, sem, value):
    if not isinstance(value, int) or value > 0:
        eng.wait_ge(sem, value)


def wait_apart(eng, passed, sem, value):
    eng.wait_ge(sem, value)
    eng.sem_inc(passed, 1)


class Chain:

    def __init__(self, eng, passed, sem, base=0):
        self.eng, self.passed, self.sem, self.base, self.n = eng, passed, sem, base, 0

    def add(self, ins):
        self.n += 1
        ins.then_inc(self.sem, 1)

    def join(self):
        wait_apart(self.eng, self.passed, self.sem, self.base + self.n)

    def __call__(self, ins):
        self.add(ins)
        self.join()


def ahead(it, j):
    return (it + j // TG, j % TG)


def peeled(eng, n, body):
    body(0, True, False)
    with eng.Fori(1, n - 1) as it:
        body(it, False, False)
    body(n - 1, False, True)


def score_banks():
    out = []
    for qt in reversed(range(NQT)):
        banks, k0 = [], KPQ * qt
        for h in range(QH):
            banks.append(([(k0, h, 0, 512, 0)], [0]))
        for h in range(QH):
            banks.append(([(k0 + 1, h, 128, 384, 0), (k0 + 3, h, 384, 128, 384)], [0, 384]))
        for h in range(0, QH, 2):
            banks.append(([(k0 + 2, h, 256, 256, 0), (k0 + 2, h + 1, 256, 256, 256)], [0, 256]))
        for kb in reversed(range(k0)):
            for h in range(QH):
                banks.append(([(kb, h, 0, 512, 0)], []))
        out.append((qt, banks))
    return out


def score_groups():
    groups = []
    for qt, banks in score_banks():
        cuts = [1] + [2] * ((len(banks) - 2) // 2) + [1]
        assert sum(cuts) == len(banks)
        at_ = 0
        for i, c in enumerate(cuts):
            groups.append((qt, banks[at_:at_ + c], i == len(cuts) - 1))
            at_ += c
    return groups


GROUPS = score_groups()
NGR = len(GROUPS)
NPB = 9
NSB = 3
LAG = 4
assert NGR % NPB == 0 and NGR % NSB == 0
HAS_TRI = [any(tri for _, tri in banks) for _, banks, _ in GROUPS]
NMASK = sum(HAS_TRI)
FIRST = {}
for _i, (_qt, _banks, _) in enumerate(GROUPS):
    for _items, _ in _banks:
        FIRST.setdefault(_items[0][0] // KPQ, _i)
LAST = {qt: i for i, (qt, _, ends) in enumerate(GROUPS) if ends}


def build(nc, x, wq, wk, wv, wo, qw, kw, cos, sin, wffn, w1s, w2s, h1s, h2s, w3s, out):
    def dram(name, shape):
        return nc.dram_tensor(name, shape, F32, kind="Internal").ap()

    qk_parts = dram("qk_parts", [2, 2, B, H * HD, T])
    neg_max = dram("neg_max", [B * H, T])
    v_second = dram("v_second", [H // QH, P, TPB, QH * HD])
    attn_t = dram("attn_t", [B, H * HD, T])
    with ExitStack() as top:
        g = Shared()
        g.passed = top.enter_context(nc.semaphore("passed"))
        g.parts_out = [top.enter_context(nc.semaphore(f"parts_out{i}")) for i in range(2)]
        g.v_out = top.enter_context(nc.semaphore("v_out"))
        g.kq_in = [top.enter_context(nc.semaphore(f"kq_in{i}")) for i in range(NQT)]

        arena = Arena(nc, -(-nc.sbuf_base // 32) * 32)
        g.ident = arena("ident", [P, P])
        g.qk_small = arena("qk_small", [P, 1], I32)
        g.w_exact = arena("w_exact", [P, 1], I32)
        g.w_diff = arena("w_diff", [P, W_CHUNKS])
        g.ones = arena("ones", [P, 1])
        g.worst = arena("worst", [P, 1])
        weights_at = arena.at
        work_at = weights_at + W_KEPT * W_CHUNK * 4
        g.Wr = Arena(nc, weights_at)("Wr", [P, W_CHUNKS, W_CHUNK], F32R)
        g.Wf = Arena(nc, weights_at)("Wf", [P, W_CHUNKS, W_CHUNK])
        work = Arena(nc, work_at)
        g.QT = work("QT", [P, QH, T], F32R)
        g.KT = work("KT", [P, QH, T], F32R)
        g.V = work("V", [P, TPB, QH, STRIP])
        second_at = work.at + NU // B * TPB * QH * HD * 4
        g.vres = work("vres", [P, NU, TPB, QH * HD])
        rest_at = work.at
        second = Arena(nc, second_at)
        g.staged = second("staged", [P, W_CHUNK])
        g.late_in = top.enter_context(nc.semaphore("late_in"))

        prep(nc, g, Arena(nc, weights_at), Arena(nc, rest_at), x, wq, wk, wv, qw, kw, cos, sin, qk_parts, neg_max,
             v_second)
        rowmax(nc, g, Arena(nc, weights_at), qk_parts, neg_max)
        after = Arena(nc, weights_at + W_CHUNKS * W_CHUNK * 4)
        g.Wo = after("Wo", [P, DC, D])
        g.S = after("S_scales", [P, 4, HC])
        g.S3 = after("S3", [P, D])
        g.at_in = after("at_in", [P, DC, QW])
        g.x_in = after("x_in", [P, TG, D])
        g.x2 = after("x2", [P, 2, TG, D])
        g.xf = after("xf", [P, TG, D])
        g.st = after("st", [P, 3, TG, 6])
        g.mv = after("mv_ffn", [P, 3, TG, 2])
        g.sd = after("sd", [P, 3, TG])
        g.rs = after("rs", [P, 3, TG])
        g.xs = after("xs", [P, 2, DC, QW], F32R)
        g.xfT = after("xfT", [P, DC, QW])
        attention(nc, g, second, x, wo, wffn, w1s, w2s, h1s, h2s, w3s, qk_parts, neg_max, v_second, attn_t)
        ffn(nc, g, after, wffn, x, attn_t, out)


def prep(nc, g, low, high, x, wq, wk, wv, qw, kw, cos, sin, qk_parts, neg_max, v_second):
    ident, vres, passed = g.ident, g.vres, g.passed
    with ExitStack() as ctx:
        s_ = high

        def ps(name, shape):
            return ctx.enter_context(nc.psum_tensor(name, shape, F32))

        def sem(name):
            return ctx.enter_context(nc.semaphore(name))

        X = low("X", [P, NT, D])
        shift = low("shift", [B * H, T])
        W = s_("W", [P, DC, 3 * D])
        C = s_("C", [P, TPB, HD // 2])
        S = s_("S", [P, TPB, HD // 2])
        nw = s_("nw", [P, 2, HD])
        nw_raw = s_("nw_raw", [P, 2, HD])
        T1 = s_("T1", [P, TPB, 2, HD])
        T2 = s_("T2", [P, TPB, 2, HD])
        eps = s_("eps", [P, 2])
        stats = s_("stats", [P, NT // 2, 6])
        mv = s_("mv", [P, NT // 2, 2])
        std = s_("std", [P, NT // 2])
        g_stats = s_("g_stats", [P, TG, 6])
        g_mv = s_("g_mv", [P, TG, 2])
        g_std = s_("g_std", [P, TG])
        rstd = s_("rstd", [P, NT])
        xn = s_("xn", [P, 2, D])
        xnT = s_("xnT", [P, 2, DC, P])
        sq = s_("sq", [P, 2, 2 * D])
        ms = s_("ms", [P, 2, 2 * H])
        rms = s_("rms", [P, 2, 2 * H])
        ri = s_("ri", [P, 2, 2 * H])
        ra = s_("ra", [P, 2, 2 * D])
        rb = s_("rb", [P, 2, 2 * D])
        rc = s_("rc", [P, 2, 2 * D])
        rd = s_("rd", [P, 2, 2 * D])
        nmr = s_("nmr", [P, NT])
        w_max = s_("w_max", [P, 2])
        w_prod = s_("w_prod", [P, 1])
        hi = low("hi", [P, 2, 4, 2 * P], F32R)
        lo = low("lo", [P, 2, 4, 2 * P], F32R)
        p_tp = [ps(f"p_tp{i}", [P, DC, P]) for i in range(2)]
        p_qk = [ps(f"p_qk{i}", [P, 2 * D]) for i in range(2)]
        p_v = [ps(f"p_v{i}", [P, D]) for i in range(2)]
        p_tq = [ps(f"p_tq{i}", [P, 4, P]) for i in range(2)]

        x_in = [sem(f"x_in{i}") for i in range(4)]
        w_in = sem("w_in")
        tab_in = sem("tab_in")
        ident_ready = sem("ident_ready")
        zeros_ready = sem("zeros_ready")
        pads_ready = sem("pads_ready")
        ones_in = sem("ones_in")
        shift_ready = sem("shift_ready")
        shift_out = sem("shift_out")
        dve_step = sem("dve_step")
        eps_ready = sem("eps_ready")
        stat_step = sem("stat_step")
        rstd_ready = sem("rstd_ready")
        norm_ready = sem("norm_ready")
        var_ready = sem("var_ready")
        std_ready = sem("std_ready")
        xn_ready = sem("xn_ready")
        xt_ready = sem("xt_ready")
        xnT_ready = sem("xnT_ready")
        qkv_ready = sem("qkv_ready")
        sq_ready = sem("sq_ready")
        v_ready = sem("v_ready")
        ms_ready = sem("ms_ready")
        rms_ready = sem("rms_ready")
        rb_ready = sem("rb_ready")
        ri_ready = sem("ri_ready")
        rc_ready = sem("rc_ready")
        rd_ready = sem("rd_ready")
        tq_ready = sem("tq_ready")
        hi_ready = sem("hi_ready")
        lo_ready = sem("lo_ready")
        parts_out, v_out = g.parts_out, g.v_out

        xv = x.rearrange("(t p) d -> p t d", p=P)
        with nc.Block() as block:
            @block.sync
            def _(sp):
                for s in range(2):
                    sp.nop().then_inc(parts_out[s], 64)
                for i in range(4):
                    n = NT // 4
                    sp.dma_start(X[:, i * n:(i + 1) * n, :], xv[:, i * n:(i + 1) * n, :]).then_inc(x_in[i], 16)
                    if i == 0:
                        for j, w in enumerate((wq, wk, wv)):
                            sp.dma_start(W[:, :, j * D:(j + 1) * D],
                                         w.rearrange("(c p) n -> p c n", p=P)).then_inc(w_in, 16)
                        sp.dma_start(C[:], cos.rearrange("(t p) d -> p t d", p=P)).then_inc(tab_in, 16)
                        sp.dma_start(S[:], sin.rearrange("(t p) d -> p t d", p=P)).then_inc(tab_in, 16)
                        sp.dma_start(nw_raw[:, 0, :], qw.partition_broadcast(P)).then_inc(tab_in, 16)
                        sp.dma_start(nw_raw[:, 1, :], kw.partition_broadcast(P)).then_inc(tab_in, 16)
                sp.wait_ge(pads_ready, 3)
                sp.dma_start(g.KT[4 * HD:ROWS, :, :].bitcast(F32),
                             g.V[0:QH].rearrange("h k n e -> h (k n e)")).then_inc(ones_in, 16)
                sp.wait_ge(shift_ready, 1)
                sp.dma_start(neg_max, shift[:]).then_inc(shift_out, 16)

                def parts(it):
                    for s in range(2):
                        for part, (buf, ready) in enumerate(((hi, hi_ready), (lo, lo_ready))):
                            sp.wait_ge(ready, at(it, TG, 2 * s + 2))
                            for qk in range(2):
                                dst = qk_parts[part, qk, it // (NG // B)].rearrange("(c p) t -> p c t", p=P)[
                                    :, :, bass.ds((it % (NG // B)) * TG * P + 2 * s * P, 2 * P)]
                                sp.dma_start(dst, buf[:, s, 2 * qk:2 * qk + 2, :].bitcast(F32)).then_inc(
                                    parts_out[s], 16)
                with sp.Fori(0, NG // B) as it:
                    parts(it)
                for s in range(2):
                    sp.wait_ge(parts_out[s], (NG // B + 1) * 64)
                sp.wait_ge(ones_in, 16)
                sp.wait_ge(shift_out, 16)
                for i, piece in enumerate(reversed(range(NQT))):
                    load_quad_piece(sp, qk_parts, g.QT, g.KT, 0, piece, g.kq_in[piece])
                    load_shift(sp, neg_max, g.QT, 0, piece, g.kq_in[piece])
                    it = NG // B + i
                    parts(it)
                    sp.wait_ge(v_ready, (it + 1) * TG)
                    keys = slice(i * TG, (i + 1) * TG)
                    sp.dma_start(v_second.rearrange("u p k e -> p u k e")[:, :, keys],
                                 vres[:, H // QH:NU, keys]).then_inc(v_out, 16)


            @block.gpsimd
            def _(pool):
                pool.memset(ident[:], 0.0).then_inc(ident_ready, 1)
                pool.memset(eps[:, 0:1], LN_EPS).then_inc(eps_ready, 1)
                pool.memset(eps[:, 1:2], RMS_EPS).then_inc(eps_ready, 1)
                pool.wait_ge(ident_ready, 1)
                pool.affine_select(out=ident[:], in_=ident[:], compare_op=ALU.not_equal, fill=1.0, base=0,
                                   pattern=[[-1, P]], channel_multiplier=1).then_inc(ident_ready, 1)
                pool.memset(shift[:], 0.0).then_inc(zeros_ready, 1)
                pool.memset(g.V[:], 1.0).then_inc(pads_ready, 1)
                pool.memset(g.KT[:].bitcast(F32), 0.0).then_inc(pads_ready, 1)
                pool.memset(g.QT[:].bitcast(F32), 0.0).then_inc(pads_ready, 1)

                def body(it, first, last):
                    for j in range(TG):
                        s = j % 2
                        pool.wait_ge(rb_ready, at(it, TG, j + 1))
                        pool.tensor_tensor(rc[:, s, :], ra[:, s, :], rb[:, s, :], ALU.add).then_inc(rc_ready, 1)
                        pool.wait_ge(rc_ready, at(it, TG, j + 1))
                        pool.wait_ge(ri_ready, at(it, TG, j + 1))
                        wait(pool, tq_ready, at(it, TG, j - 1))
                        pool.tensor_tensor(rd[:, s, :].rearrange("p (g d) -> p g d", d=HD),
                                           rc[:, s, :].rearrange("p (g d) -> p g d", d=HD),
                                           ri[:, s, :].unsqueeze(2).to_broadcast([P, 2 * H, HD]),
                                           ALU.mult).then_inc(rd_ready, 1)
                peeled(pool, NG, body)

            @block.scalar
            def _(act):
                def half_std(half):
                    ts = slice(2 * half * TG, 2 * (half + 1) * TG)
                    act.wait_ge(var_ready, half + 1)
                    nc.scalar.activation(std[:, ts], mv[:, ts, 1], ACT.Sqrt, bias=eps[:, 0:1]).then_inc(std_ready, 1)
                act.wait_ge(eps_ready, 2)
                half_std(0)

                def put_xn(it, j):
                    s, t = j % 2, it * TG + j
                    wait(act, xt_ready, at(it, TG, j - 1))
                    nc.scalar.activation(xn[:, s, :], X[:, t, :], ACT.Identity, bias=nmr[:, bass.ds(t, 1)],
                                         scale=rstd[:, bass.ds(t, 1)]).then_inc(xn_ready, 1)

                def put_xnT(it, j):
                    s = j % 2
                    act.wait_ge(xt_ready, at(it, TG, j + 1))
                    wait(act, qkv_ready, at(it, TG, j - 1))
                    nc.scalar.copy(xnT[:, s], p_tp[s][:]).then_inc(xnT_ready, 1)

                def put_hi(it, j):
                    s, h = j % 2, j // 2
                    act.wait_ge(tq_ready, at(it, TG, j + 1))
                    act.wait_ge(parts_out[h], at(it, 64, 64))
                    nc.scalar.copy(hi[:, h, :, (j % 2) * P:(j % 2 + 1) * P], p_tq[s][:]).then_inc(hi_ready, 1)

                def body(it, first, last, stats_ahead):
                    for j in range(TG):
                        s = j % 2
                        if j == TG - 2 and not last:
                            act.wait_ge(norm_ready, it + 1 if first or stats_ahead else it)
                        if not (last and j >= TG - 2):
                            put_xn(*ahead(it, j + 2))
                        if not (last and j == TG - 1):
                            put_xnT(*ahead(it, j + 1))
                        act.wait_ge(qkv_ready, at(it, TG, j + 1))
                        wait(act, ms_ready, at(it, TG, j - 1))
                        nc.scalar.activation(sq[:, s, :], p_qk[s][:], ACT.Square).then_inc(sq_ready, 1)
                        nc.scalar.copy(
                            vres[:, bass.ds((it // (NG // B)) * (H // QH), H // QH),
                                 (it % (NG // B)) * TG + j, :],
                            p_v[s][:].rearrange("p (u e) -> p u e", e=QH * HD)).then_inc(v_ready, 1)
                        act.wait_ge(ms_ready, at(it, TG, j + 1))
                        wait(act, ri_ready, at(it, TG, j - 1))
                        nc.scalar.activation(rms[:, s, :], ms[:, s, :], ACT.Sqrt, bias=eps[:, 1:2],
                                             scale=1.0 / HD).then_inc(rms_ready, 1)
                        if stats_ahead and j == 2:
                            act.wait_ge(var_ready, it + 2)
                            nc.scalar.activation(g_std[:], g_mv[:, :, 1], ACT.Sqrt, bias=eps[:, 0:1]).then_inc(std_ready, 1)
                        if not (first and j < 2):
                            put_hi(*ahead(it, j - 2))
                act.wait_ge(norm_ready, 1)
                put_xn(0, 0)
                put_xn(0, 1)
                put_xnT(0, 0)
                half_std(1)
                body(0, True, False, False)
                with act.Fori(1, NG - 3) as it:
                    body(it, False, False, True)
                with act.Fori(NG - 3, NG - 1) as it:
                    body(it, False, False, False)
                body(NG - 1, False, True, False)
                put_hi(NG - 1, TG - 2)
                put_hi(NG - 1, TG - 1)

            @block.vector
            def _(dve):
                step = Chain(dve, passed, dve_step)

                def half_stats(half):
                    ts = slice(2 * half * TG, 2 * (half + 1) * TG)
                    dve.wait_ge(x_in[half], 16)
                    for t in range(ts.start, ts.stop):
                        step.add(nc.vector.bn_stats(stats[:, t, :], X[:, t, :]))
                    step.join()
                    for t in range(ts.start, ts.stop):
                        step.add(nc.vector.bn_aggr(mv[:, t, :], stats[:, t, :]))
                    step.join()
                    dve.nop().then_inc(var_ready, 1)
                    dve.wait_ge(std_ready, half + 1)
                    step(nc.vector.reciprocal(rstd[:, ts], std[:, ts]))
                    nc.vector.scalar_tensor_tensor(out=nmr[:, ts], in0=mv[:, ts, 0], scalar=-1.0, in1=rstd[:, ts],
                                                   op0=ALU.mult, op1=ALU.mult).then_inc(norm_ready, 1)
                half_stats(0)
                dve.wait_ge(tab_in, 64)
                step(nc.vector.tensor_scalar(nw[:, 0, :], nw_raw[:, 0, :], HD ** -0.5, None, ALU.mult))
                step(nc.vector.tensor_copy(nw[:, 1, :], nw_raw[:, 1, :]))
                half = HD // 2
                for qk in range(2):
                    for a in range(2):
                        own = nw[:, qk, a * half:(a + 1) * half].unsqueeze(1).to_broadcast([P, TPB, half])
                        other = nw[:, qk, (1 - a) * half:(2 - a) * half].unsqueeze(1).to_broadcast([P, TPB, half])
                        dst = slice(a * half, (a + 1) * half)
                        step(nc.vector.tensor_tensor(T1[:, :, qk, dst], C[:], own, ALU.mult))
                        step(nc.vector.scalar_tensor_tensor(out=T2[:, :, qk, dst], in0=S[:],
                                                            scalar=1.0 if a else -1.0, in1=other,
                                                            op0=ALU.mult, op1=ALU.mult))
                half_stats(1)
                step(nc.vector.tensor_reduce(w_max[:], nw[:], AX.X, ALU.max, apply_absolute_value=True))
                step(nc.vector.tensor_tensor(w_prod[:], w_max[:, 0:1], w_max[:, 1:2], ALU.mult))
                step(nc.vector.tensor_scalar(g.qk_small[:], w_prod[:], MAX_SCORE / HD, None, ALU.is_le))
                step(nc.vector.tensor_scalar(w_prod[:], w_prod[:], float(HD), None, ALU.mult))
                dve.wait_ge(zeros_ready, 1)
                nc.vector.tensor_scalar(shift[:], shift[:], w_prod[0:B * H, 0:1], None,
                                        ALU.subtract).then_inc(shift_ready, 1)

                def put_lo(it, j):
                    s, h = j % 2, j // 2
                    dve.wait_ge(hi_ready, at(it, TG, j + 1))
                    dve.wait_ge(parts_out[h], at(it, 64, 64))
                    nc.vector.tensor_tensor(lo[:, h, :, (j % 2) * P:(j % 2 + 1) * P], p_tq[s][:],
                                            hi[:, h, :, (j % 2) * P:(j % 2 + 1) * P].bitcast(F32),
                                            ALU.subtract).then_inc(lo_ready, 1)

                def group_stats(it, j):
                    if j < 2:
                        for i in (2 * j, 2 * j + 1):
                            nc.vector.bn_stats(g_stats[:, i, :], X[:, (it + 3) * TG + i, :]).then_inc(stat_step, 1)
                    elif j == 2:
                        wait_apart(dve, passed, stat_step, at(it - 1, 2 * TG, TG))
                        for i in range(TG):
                            nc.vector.bn_aggr(g_mv[:, i, :], g_stats[:, i, :]).then_inc(stat_step, 1)
                        wait_apart(dve, passed, stat_step, at(it - 1, 2 * TG, 2 * TG))
                        dve.nop().then_inc(var_ready, 1)
                    else:
                        ts = bass.ds((it + 3) * TG, TG)
                        dve.wait_ge(std_ready, it + 2)
                        nc.vector.reciprocal(rstd[:, ts], g_std[:]).then_inc(rstd_ready, 1)
                        wait_apart(dve, passed, rstd_ready, it)
                        nc.vector.scalar_tensor_tensor(out=nmr[:, ts], in0=g_mv[:, :, 0], scalar=-1.0, in1=rstd[:, ts],
                                                       op0=ALU.mult, op1=ALU.mult).then_inc(norm_ready, 1)
                        wait_apart(dve, passed, norm_ready, it + 2)

                def body(it, first, last, stats_ahead):
                    for j in range(TG):
                        s = j % 2
                        if stats_ahead:
                            group_stats(it, j)
                        pos = (it % (NG // B)) * TG + j
                        dve.wait_ge(sq_ready, at(it, TG, j + 1))
                        wait(dve, rms_ready, at(it, TG, j - 1))
                        nc.vector.tensor_reduce(ms[:, s, :], sq[:, s, :].rearrange("p (g d) -> p g d", d=HD),
                                                AX.X, ALU.add).then_inc(ms_ready, 1)
                        wait(dve, rc_ready, at(it, TG, j - 1))
                        dve.wait_ge(sq_ready, at(it, TG, j + 1))
                        qk4 = p_qk[s][:].rearrange("p (k h d) -> p k h d", k=2, d=HD)
                        ra4 = ra[:, s, :].rearrange("p (k h d) -> p k h d", k=2, d=HD)
                        rb4 = rb[:, s, :].rearrange("p (k h d) -> p k h d", k=2, d=HD)
                        nc.vector.tensor_tensor(ra4, qk4, T1[:, pos].unsqueeze(2).to_broadcast([P, 2, H, HD]),
                                                ALU.mult)
                        for a in range(2):
                            ins = nc.vector.tensor_tensor(
                                rb4[:, :, :, a * half:(a + 1) * half], qk4[:, :, :, (1 - a) * half:(2 - a) * half],
                                T2[:, pos, :, a * half:(a + 1) * half].unsqueeze(2).to_broadcast([P, 2, H, half]),
                                ALU.mult)
                        ins.then_inc(rb_ready, 1)
                        dve.wait_ge(rms_ready, at(it, TG, j + 1))
                        wait(dve, rd_ready, at(it, TG, j - 1))
                        nc.vector.reciprocal(ri[:, s, :], rms[:, s, :]).then_inc(ri_ready, 1)
                        if not (first and j < 2):
                            put_lo(*ahead(it, j - 2))
                body(0, True, False, False)
                dve.wait_ge(x_in[2], 16)
                dve.wait_ge(x_in[3], 16)
                with dve.Fori(1, NG - 3) as it:
                    body(it, False, False, True)
                with dve.Fori(NG - 3, NG - 1) as it:
                    body(it, False, False, False)
                body(NG - 1, False, True, False)
                put_lo(NG - 1, TG - 2)
                put_lo(NG - 1, TG - 1)

            @block.tensor
            def _(pe):
                pe.wait_ge(ident_ready, 2)

                def turn_x(it, j):
                    s = j % 2
                    pe.wait_ge(xn_ready, at(it, TG, j + 1))
                    wait(pe, xnT_ready, at(it, TG, j - 1))
                    for c in range(DC):
                        ins = pe.transpose(p_tp[s][:, c, :], xn[:, s, c * P:(c + 1) * P], ident[:])
                    ins.then_inc(xt_ready, 1)

                def turn_qk(it, j):
                    s = j % 2
                    pe.wait_ge(rd_ready, at(it, TG, j + 1))
                    wait(pe, lo_ready, at(it, TG, j - 1))
                    for c in range(4):
                        ins = pe.transpose(p_tq[s][:, c, :], rd[:, s, c * P:(c + 1) * P], ident[:])
                    ins.then_inc(tq_ready, 1)

                def body(it, first, last):
                    for j in range(TG):
                        s = j % 2
                        if not (last and j == TG - 1):
                            turn_x(*ahead(it, j + 1))
                        pe.wait_ge(xnT_ready, at(it, TG, j + 1))
                        wait(pe, rb_ready, at(it, TG, j - 1))
                        for c in range(DC):
                            pe.matmul(p_qk[s][:], xnT[:, s, c, :], W[:, c, 0:2 * D], start=(c == 0),
                                      stop=(c == DC - 1))
                        wait(pe, v_ready, at(it, TG, j - 1))
                        for c in range(DC):
                            ins = pe.matmul(p_v[s][:], xnT[:, s, c, :], W[:, c, 2 * D:3 * D], start=(c == 0),
                                            stop=(c == DC - 1))
                        ins.then_inc(qkv_ready, 1)
                        if not (first and j < 2):
                            turn_qk(*ahead(it, j - 2))
                turn_x(0, 0)
                pe.wait_ge(w_in, 48)
                peeled(pe, NG, body)
                turn_qk(NG - 1, TG - 2)
                turn_qk(NG - 1, TG - 1)


def wait_prep_out(eng, g):
    for s in range(2):
        eng.wait_ge(g.parts_out[s], (NG + 1) * 64)
    eng.wait_ge(g.v_out, NQT * 16)


def load_quad_piece(sp, qk_parts, QT, KT, u, piece, landed):
    b, quad = u // (H // QH), u % (H // QH)
    for side, rows in ((0, (0, 0, 1, 1)), (1, (0, 1, 0, 1))):
        for r, part in enumerate(rows):
            src = qk_parts[part, side, b].rearrange("(q h d) t -> q d h t", h=QH, d=HD)[
                quad, :, :, piece * QW:(piece + 1) * QW]
            dst = (QT, KT)[side][r * HD:(r + 1) * HD, :, piece * QW:(piece + 1) * QW].bitcast(F32)
            sp.dma_start(dst, src).then_inc(landed, 16)


def load_shift(sp, neg_max, QT, u, piece, landed):
    src = neg_max.rearrange("(u o h) t -> u o h t", h=QH, o=1)[u, :, :, piece * QW:(piece + 1) * QW]
    sp.dma_start(QT[4 * HD:ROWS, :, piece * QW:(piece + 1) * QW].bitcast(F32), src).then_inc(landed, 16)


def rowmax(nc, g, s_, qk_parts, neg_max):
    QT, KT, ident, passed = g.QT, g.KT, g.ident, g.passed
    with ExitStack() as ctx:
        def sem(name):
            return ctx.enter_context(nc.semaphore(name))

        ident_r = s_("ident_r", [P, P], F32R)
        future_f = s_("future_f", [P, P])
        future = s_("future", [P, P], F32R)
        mx = s_("mx", [P, QH * TPB])
        neg = s_("neg", [QH * TPB, P], F32R)
        p_s = [ctx.enter_context(nc.psum_tensor(f"p_s{i}", [P, T], F32)) for i in range(2)]
        loaded = sem("loaded")
        shift_in = sem("shift_in")
        consts = sem("consts")
        consts_r = sem("consts_r")
        rows_ready = sem("rows_ready")
        mx_ready = sem("mx_ready")
        turned = sem("turned")
        neg_ready = sem("neg_ready")
        neg_out = sem("neg_out")
        NR = QH * TPB
        NLOAD = 8 * NQT * 16

        def unbounded(eng):
            return eng.If(eng.value_load(g.qk_small[0:1, 0:1], min_val=0, max_val=1) == 0)

        with nc.Block() as block:
            @block.sync
            def _(sp):
                with unbounded(sp):
                    wait_prep_out(sp, g)
                    for piece in range(NQT):
                        load_quad_piece(sp, qk_parts, QT, KT, 0, piece, loaded)
                    with sp.Fori(0, NU) as u:
                        wait_apart(sp, passed, turned, u + 1)
                        for piece in range(NQT):
                            load_quad_piece(sp, qk_parts, QT, KT, (u + 1) % NU, piece, loaded)
                        wait_apart(sp, passed, neg_ready, u + 1)
                        sp.dma_start(neg_max.rearrange("(u h) (t p) -> u (h t) p", h=QH, p=P)[u],
                                     neg[:].bitcast(F32)).then_inc(neg_out, 16)
                    sp.wait_ge(neg_out, NU * 16)
                    sp.wait_ge(loaded, (NU + 1) * NLOAD)
                    for piece in range(NQT):
                        load_shift(sp, neg_max, QT, 0, piece, shift_in)
                    sp.wait_ge(shift_in, NQT * 16)

            @block.gpsimd
            def _(pool):
                with unbounded(pool):
                    pool.memset(future_f[:], 0.0).then_inc(consts, 1)
                    pool.wait_ge(consts, 1)
                    pool.affine_select(out=future_f[:], in_=future_f[:], compare_op=ALU.is_ge, fill=MASKED, base=0,
                                       pattern=[[-1, P]], channel_multiplier=1).then_inc(consts, 1)

            @block.tensor
            def _(pe):
                with unbounded(pe):
                    pe.wait_ge(consts_r, 2)
                    with pe.Fori(0, NU) as u:
                        pe.wait_ge(loaded, at(u, NLOAD, NLOAD))
                        for n in range(NR):
                            h, qb = n // TPB, n % TPB
                            buf = p_s[n % 2]
                            pe.wait_ge(mx_ready, at(u, NR, n + 1))
                            keys = (qb + 1) * P
                            q = QT[0:4 * HD, h, qb * P:(qb + 1) * P]
                            for k0 in range(0, keys - P, QW):
                                k1 = min(k0 + QW, keys - P)
                                pe.matmul(buf[:, k0:k1], q, KT[0:4 * HD, h, k0:k1], start=True, stop=True)
                            pe.matmul(buf[:, keys - P:keys], q, KT[0:4 * HD, h, keys - P:keys], start=True, stop=False)
                            pe.matmul(buf[:, keys - P:keys], ident_r[:], future[:], start=False,
                                      stop=True).then_inc(rows_ready, 1)
                        wait_apart(pe, passed, mx_ready, at(u, NR, NR + 2))
                        pe.transpose(p_s[0][0:NR, 0:P], mx[:], ident[:]).then_inc(turned, 1)
                        pe.wait_ge(neg_ready, u + 1)

            @block.vector
            def _(dve):
                with unbounded(dve):
                    dve.wait_ge(consts, 2)
                    nc.vector.tensor_copy(future[:], future_f[:]).then_inc(consts_r, 1)
                    nc.vector.tensor_copy(ident_r[:], ident[:]).then_inc(consts_r, 1)
                    dve.nop().then_inc(mx_ready, 2)
                    with dve.Fori(0, NU) as u:
                        for n in range(NR):
                            keys = (n % TPB + 1) * P
                            dve.wait_ge(rows_ready, at(u, NR, n + 1))
                            nc.vector.tensor_reduce(mx[:, n:n + 1], p_s[n % 2][:, 0:keys], AX.X,
                                                    ALU.max).then_inc(mx_ready, 1)
                        dve.wait_ge(turned, u + 1)
                        nc.vector.tensor_scalar(neg[:], p_s[0][0:NR, 0:P], -1.0, None, ALU.mult).then_inc(neg_ready, 1)
                        dve.wait_ge(neg_out, at(u, 16, 16))


def late_chunks(g):
    at_v = [g.vres[:, i:i + 2].rearrange("p u k e -> p (u k e)") for i in (0, 2)]
    return at_v + [g.staged[:]]


def attention(nc, g, s_, x, wo, wffn, w1s, w2s, h1s, h2s, w3s, qk_parts, neg_max, v_second, attn_t):
    QT, KT, V, vres, kq_in, staged, passed = g.QT, g.KT, g.V, g.vres, g.kq_in, g.staged, g.passed
    with ExitStack() as ctx:
        def sem(name):
            return ctx.enter_context(nc.semaphore(name))

        o_sb = [s_(f"o_sb{i}", [P, QW]) for i in range(2)]
        den = s_("den", [P, QW])
        o_norm = [s_(f"o_norm{i}", [P, QW]) for i in range(2)]
        probs = [s_(f"probs{i}", [P, 2 * QW]) for i in range(NPB)]
        p_s = [ctx.enter_context(nc.psum_tensor(f"p_sc{i}", [P, 2 * QW], F32)) for i in range(NSB)]
        p_o = [ctx.enter_context(nc.psum_tensor(f"p_o{i}", [P, QW], F32)) for i in range(2)]

        w_in = sem("w_staged")
        late_in = sem("late_staged")
        late_step = sem("late_step")
        v_loaded = sem("v_loaded")
        w_step = sem("w_step")
        v_in = sem("v_in")
        scores_ready = sem("scores_ready")
        probs_ready = sem("probs_ready")
        masked = sem("masked")
        probs_used = sem("probs_used")
        o_copied = sem("o_copied")
        den_ready = sem("den_ready")
        rden_ready = sem("rden_ready")
        o_ready = sem("o_ready")
        o_out = [sem(f"o_out{i}") for i in range(2)]
        NDMA = 9 * 16
        first = mix_first(nc, g, ctx, x, wo, w1s, w2s, h1s, h2s, w3s, attn_t,
                          [p_s[0][:, 0:QW], p_s[0][:, QW:2 * QW]], p_s[1][:, 0:1])

        with nc.Block() as block:
            @block.sync
            def _(sp):
                for s in range(2):
                    sp.nop().then_inc(o_out[s], 64)
                wait_prep_out(sp, g)

                def body(u, last, load_v=False, check_late=False):
                    b, quad = u // (H // QH), u % (H // QH)
                    wait_apart(sp, passed, w_step, at(u, 3, 3))
                    if check_late:
                        sp.dma_start(staged[:], wffn[W_KEPT + u % N_LATE]).then_inc(late_in, 16)
                    else:
                        sp.dma_start(staged[:], wffn[u]).then_inc(w_in, 16)
                    for i, piece in enumerate(reversed(range(NQT))):
                        if not last:
                            wait_apart(sp, passed, scores_ready, at(u, NGR, LAST[piece] + 1))
                            load_quad_piece(sp, qk_parts, QT, KT, u + 1, piece, kq_in[piece])
                            load_shift(sp, neg_max, QT, u + 1, piece, kq_in[piece])
                        if check_late and i == 1:
                            wait_apart(sp, passed, late_step, at(u, 3, 3))
                            sp.dma_start(staged[:], wffn[u]).then_inc(w_in, 16)
                        if i == 1 and last:
                            sp.wait_ge(v_in, NU * NQT)
                            for n, dst in enumerate(late_chunks(g)[:2]):
                                sp.dma_start(dst, wffn[W_KEPT + n]).then_inc(g.late_in, 16)
                        if i == 2 and last:
                            sp.wait_ge(w_step, (NU + 1) * 3)
                            sp.dma_start(staged[:], wffn[W_CHUNKS - 1]).then_inc(g.late_in, 16)
                        wait_apart(sp, passed, o_ready, at(u, NQT, i + 1))
                        for h in range(QH):
                            sp.dma_start(attn_t[b].rearrange("(q h d) t -> q h d t", h=QH, d=HD)[
                                quad, h, :, piece * QW:(piece + 1) * QW],
                                o_norm[i % 2][h * STRIP:h * STRIP + HD, :]).then_inc(o_out[i % 2], 16)
                    if load_v:
                        wait_apart(sp, passed, v_in, at(u, NQT, NQT))
                        sp.dma_start(vres[:, u], v_second[u]).then_inc(v_loaded, 16)
                with sp.Fori(0, H // QH) as u:
                    body(u, False, load_v=True, check_late=True)
                with sp.Fori(H // QH, NU - 1) as u:
                    body(u, False)
                body(NU - 1, True)
                first.sync(sp)
                for s in range(2):
                    sp.wait_ge(o_out[s], (NU * NQT // 2 + 1) * 64)

            @block.gpsimd
            def _(pool):
                def put_v(u, piece):
                    nc.gpsimd.tensor_copy(V[:, piece * KPQ:(piece + 1) * KPQ, :, 0:HD],
                                          vres[:, u % (H // QH), piece * KPQ:(piece + 1) * KPQ, :].rearrange(
                                              "p k (h d) -> p k h d", d=HD)).then_inc(v_in, 1)

                for piece in reversed(range(NQT)):
                    put_v(0, piece)

                def mask(buf, kinds):
                    b0 = 0
                    while b0 < len(kinds):
                        tri, m = kinds[b0], b0 + 1
                        if len(tri) == 1:
                            while m < len(kinds) and kinds[m] == tri:
                                m += 1
                            v = buf[:, b0 * QW:m * QW].rearrange("p (n c) -> p n c", c=QW)[:, :, 0:P]
                        elif tri:
                            v = buf[:, b0 * QW:m * QW].rearrange("p (a c) -> p a c", c=P)[
                                :, 0:tri[1] // P + 1:tri[1] // P, :]
                        if tri:
                            ins = nc.gpsimd.affine_select(out=v, in_=v, compare_op=ALU.is_ge, fill=0.0, base=0,
                                                          pattern=[[0, v.shape[1]], [1, P]],
                                                          channel_multiplier=-1)
                        b0 = m
                    return ins

                def body(u, first, last, second):
                    n = 0
                    for i, (qt, banks, ends) in enumerate(GROUPS):
                        if HAS_TRI[i]:
                            n += 1
                            wait_apart(pool, passed, probs_ready, at(u, NGR, i + 1 + NSB))
                            mask(probs[i % NPB], [tuple(tri) for _, tri in banks]).then_inc(masked, 1)
                            if not HAS_TRI[(i + 1) % NGR] or GROUPS[(i + 1) % NGR][0] != qt:
                                if not first and qt == NQT - 1:
                                    wait_apart(pool, passed, probs_used, at(u, NGR, NPB))
                                    put_v(u, 0)
                                if not last and qt < NQT - 1:
                                    wait_apart(pool, passed, probs_used, at(u, NGR, LAST[qt + 1] + 1 + NPB))
                                    if second:
                                        pool.wait_ge(v_loaded, at(u, 16, 32 - (H // QH) * 16))
                                    put_v(u + 1, qt + 1)
                body(0, True, False, False)
                with pool.Fori(1, H // QH - 1) as u:
                    body(u, False, False, False)
                with pool.Fori(H // QH - 1, NU - 1) as u:
                    body(u, False, False, True)
                body(NU - 1, False, True, False)
                first.gpsimd(pool)

            @block.scalar
            def _(act):
                act.nop().then_inc(probs_ready, NSB)
                with act.Fori(0, NU) as u:
                    for i, (qt, banks, ends) in enumerate(GROUPS):
                        n = len(banks) * QW
                        act.wait_ge(scores_ready, at(u, NGR, i + 1))
                        act.wait_ge(probs_used, at(u, NGR, i + 1))
                        nc.scalar.activation(probs[i % NPB][:, 0:n], p_s[i % NSB][:, 0:n],
                                             ACT.Exp).then_inc(probs_ready, 1)
                act.wait_ge(scores_ready, NU * NGR)
                for s in range(2):
                    act.wait_ge(o_out[s], (NU // B * NQT // 2 + 1) * 64)
                first.scalar(act)

            @block.tensor
            def _(pe):
                pe.nop().then_inc(probs_used, NPB)

                def scores(u, i):
                    qt, banks, _ = GROUPS[i]
                    for piece in range(NQT):
                        if i == FIRST[piece]:
                            pe.wait_ge(kq_in[piece], at(u, NDMA, NDMA))
                    pe.wait_ge(probs_ready, at(u, NGR, i + 1))
                    for n, (items, _) in enumerate(banks):
                        for kb, h, q0, w, c in items:
                            ins = pe.matmul(p_s[i % NSB][:, n * QW + c:n * QW + c + w],
                                            KT[:, h, kb * P:(kb + 1) * P],
                                            QT[:, h, qt * QW + q0:qt * QW + q0 + w],
                                            start=True, stop=True)
                    ins.then_inc(scores_ready, 1)

                def values(u, i):
                    qt, banks, ends = GROUPS[i]
                    order = NQT - 1 - qt
                    if i == 0 or GROUPS[i - 1][0] != qt:
                        pe.wait_ge(o_copied, at(u, NQT, order + 1))
                    if qt == NQT - 1:
                        piece = min(kb for items, _ in banks for kb, *_ in items) // KPQ
                        pe.wait_ge(v_in, at(u, NQT, NQT - piece))
                    pe.wait_ge(probs_ready, at(u, NGR, i + 1 + NSB))
                    if HAS_TRI[i]:
                        pe.wait_ge(masked, at(u, NMASK, sum(HAS_TRI[:i + 1])))
                    for n, (items, _) in enumerate(banks):
                        for kb, h, q0, w, c in items:
                            ins = pe.matmul(p_o[order % 2][h * STRIP:(h + 1) * STRIP, q0:q0 + w],
                                            V[:, kb, h, :], probs[i % NPB][:, n * QW + c:n * QW + c + w],
                                            start=(kb == KPQ * qt), stop=(kb == (0 if qt else 3)),
                                            skip_group_check=True)
                    ins.then_inc(probs_used, 1)

                def body(u, first, last):
                    for i in range(0, NGR, 2):
                        for k in range(i, i + 2):
                            if k + NSB < NGR:
                                scores(u, k + NSB)
                            elif not last:
                                scores(u + 1, k + NSB - NGR)
                        for k in range(i, i + 2):
                            if k >= LAG:
                                values(u, k - LAG)
                            elif not first:
                                values(u - 1, NGR + k - LAG)
                for i in range(NSB):
                    scores(0, i)
                peeled(pe, NU, body)
                for i in range(LAG):
                    values(NU - 1, NGR - LAG + i)
                pe.wait_ge(probs_ready, NU * NGR + NSB)
                first.tensor(pe)

            @block.vector
            def _(dve):
                dve.nop().then_inc(o_copied, 2)
                dve.wait_ge(g.v_out, NQT * 16)

                dve.nop().then_inc(w_step, 3)

                def round_weights(u, loaded, step, base, column):
                    wait_apart(dve, passed, loaded, at(u, 16, 16))
                    nc.vector.tensor_copy(g.Wr[:, u, :], staged[:]).then_inc(step, 1)
                    dve.wait_ge(step, at(u, 3, base + 1))
                    nc.vector.tensor_tensor(staged[:], staged[:], g.Wr[:, u, :].bitcast(F32),
                                            ALU.subtract).then_inc(step, 1)
                    dve.wait_ge(step, at(u, 3, base + 2))
                    nc.vector.tensor_reduce(g.w_diff[:, bass.ds(column, 1)], staged[:], AX.X, ALU.max,
                                            apply_absolute_value=True).then_inc(step, 1)

                def body(u, check_late):
                    for i, qt in enumerate(reversed(range(NQT))):
                        dve.wait_ge(probs_used, at(u, NGR, LAST[qt] + 1 + NPB))
                        nc.vector.tensor_copy(o_sb[i % 2][:], p_o[i % 2][:]).then_inc(o_copied, 1)
                        wait_apart(dve, passed, o_copied, at(u, NQT, i + 1 + 2))
                        nc.vector.stream_shuffle(den[:], o_sb[i % 2][:], [HD] * STRIP).then_inc(den_ready, 1)
                        dve.wait_ge(den_ready, at(u, NQT, i + 1))
                        nc.vector.reciprocal(den[:], den[:]).then_inc(rden_ready, 1)
                        dve.wait_ge(rden_ready, at(u, NQT, i + 1))
                        dve.wait_ge(o_out[i % 2], at(u, 128, 64 * (i // 2) + 64))
                        nc.vector.tensor_tensor(o_norm[i % 2][:], o_sb[i % 2][:], den[:], ALU.mult).then_inc(o_ready, 1)
                        if i == 0 and check_late:
                            round_weights(u, late_in, late_step, 0, W_KEPT + u % N_LATE)
                            wait_apart(dve, passed, late_step, at(u, 3, 3))
                        if i == (1 if check_late else 0):
                            round_weights(u, w_in, w_step, 3, u)
                with dve.Fori(0, H // QH) as u:
                    body(u, True)
                with dve.Fori(H // QH, NU) as u:
                    body(u, False)
                dve.wait_ge(w_step, (NU + 1) * 3)
                first.vector(dve)


def load_at(eng, g, attn_t, turn, landed):
    eng.dma_start(g.at_in[:], attn_t[turn // (NG // B)].rearrange("(c p) t -> p c t", p=P)[
        :, :, bass.ds((turn % (NG // B)) * QW, QW)]).then_inc(landed, 16)


def load_x(eng, g, x, turn, landed):
    eng.dma_start(g.x_in[:], x.rearrange("(g t p) d -> g p t d", t=TG, p=P)[turn]).then_inc(landed, 16)


def project(pe, g, banks, y_made):
    for j in range(TG):
        for c in range(DC):
            ins = pe.matmul(banks[j // 2][:, (j % 2) * D:(j % 2 + 1) * D], g.at_in[:, c, j * P:(j + 1) * P],
                            g.Wo[:, c, :], start=(c == 0), stop=(c == DC - 1))
        ins.then_inc(y_made, 1)


def turn_xf(pe, g, banks, xt_ready):
    for j in range(TG):
        for c in range(DC):
            col = ((j % 2) * DC + c) * P
            ins = pe.transpose(banks[j // 2][:, col:col + P], g.xf[:, j, c * P:(c + 1) * P], g.ident[:])
        if j % 2:
            ins.then_inc(xt_ready, 1)


def by_token(t, b):
    return t.rearrange("p c (b j t) -> p b j c t", b=2, j=2)[:, b]


def bank_tokens(bank):
    return bank.rearrange("p (j c t) -> p j c t", j=2, c=DC)


def split_xf(nc, dve, g, b, bank, ready, before):
    hi, lo = by_token(g.xs[:, 0], b), by_token(g.xs[:, 1], b)
    nc.vector.tensor_copy(hi, bank_tokens(bank)).then_inc(ready, 1)
    dve.wait_ge(ready, before + 1)
    nc.vector.tensor_tensor(lo, bank_tokens(bank), hi.bitcast(F32), ALU.subtract).then_inc(ready, 1)


def ln_stats(nc, g, step, n, tile, var_ready):
    for j in range(TG):
        step.add(nc.vector.bn_stats(g.st[:, n, j], tile(j)))
    step.join()
    for j in range(TG):
        step.add(nc.vector.bn_aggr(g.mv[:, n, j], g.st[:, n, j]))
    step.join()
    nc.vector.tensor_scalar(g.mv[:, n, :, 1], g.mv[:, n, :, 1], LN_EPS, None, ALU.add).then_inc(var_ready, 1)


def ln_apply(nc, g, step, n, tile, out):
    step(nc.vector.reciprocal(g.rs[:, n], g.sd[:, n]))
    for j in range(TG):
        step.add(nc.vector.tensor_scalar(out(j), tile(j), g.mv[:, n, j, 0:1], g.rs[:, n, j:j + 1],
                                         ALU.subtract, ALU.mult))


MIX_STEPS = 2 * TG + 1 + TG + 1 + 2 * TG + 1 + TG
MIX_X2 = 2 * TG + 1 + TG + 1


def mix_first(nc, g, ctx, x, wo, w1s, w2s, h1s, h2s, w3s, attn_t, banks, p_flag):
    passed, ones, worst = g.passed, g.ones, g.worst
    late = late_chunks(g)

    def sem(name):
        return ctx.enter_context(nc.semaphore(name))

    wo_in = sem("wo_in")
    at_in = sem("at_in_m")
    x_in = sem("x_in_m")
    s_in = sem("s_in")
    split = sem("split_m")
    ones_ready = sem("ones_m")
    worst_ready = sem("worst_ready")
    summed = sem("summed")
    y_made = sem("y_made_m")
    step_m = sem("step_m")
    var_ready = sem("var_m")
    std_ready = sem("std_m")
    xt_ready = sem("xt_m")

    def sync(sp):
        for i, w in enumerate((w1s, w2s, h1s, h2s)):
            sp.dma_start(g.S[:, i, :], w).then_inc(s_in, 16)
        sp.dma_start(g.S3[:], w3s.partition_broadcast(P)).then_inc(s_in, 16)
        sp.wait_ge(s_in, 5 * 16)

    def tensor(pe):
        pe.wait_ge(wo_in, 16)
        pe.wait_ge(at_in, 16)
        project(pe, g, banks, y_made)
        pe.wait_ge(worst_ready, 1)
        pe.wait_ge(ones_ready, 1)
        pe.matmul(p_flag[0:1, 0:1], worst[:], ones[:], start=True, stop=True).then_inc(summed, 1)
        pe.wait_ge(step_m, MIX_STEPS)
        turn_xf(pe, g, banks, xt_ready)

    def gpsimd(pool):
        pool.memset(ones[:], 1.0).then_inc(ones_ready, 1)

    def scalar(act):
        load_at(act, g, attn_t, 0, at_in)
        act.dma_start(g.Wo[:], wo.rearrange("(c p) n -> p c n", p=P)).then_inc(wo_in, 16)
        load_x(act, g, x, 0, x_in)
        act.wait_ge(g.late_in, N_LATE * 16)
        for i in range(N_LATE):
            nc.scalar.copy(g.Wr[:, W_KEPT + i, :], late[i])
        for n in range(2):
            act.wait_ge(var_ready, n + 1)
            nc.scalar.activation(g.sd[:, n], g.mv[:, n, :, 1], ACT.Sqrt).then_inc(std_ready, 1)

    def vector(dve):
        step = Chain(dve, passed, step_m)

        def y(j):
            return banks[j // 2][:, (j % 2) * D:(j % 2 + 1) * D]

        def x2(j):
            return g.x2[:, 0, j]

        nc.vector.tensor_reduce(worst[:], g.w_diff[:], AX.X, ALU.max).then_inc(worst_ready, 1)
        dve.wait_ge(y_made, TG)
        ln_stats(nc, g, step, 0, y, var_ready)
        dve.wait_ge(std_ready, 1)
        ln_apply(nc, g, step, 0, y, x2)
        dve.wait_ge(x_in, 16)
        step.join()
        step(nc.vector.tensor_tensor(g.x2[:, 0], g.x2[:, 0], g.x_in[:], ALU.add))
        assert step.n == MIX_X2
        ln_stats(nc, g, step, 1, x2, var_ready)
        dve.wait_ge(summed, 1)
        nc.vector.tensor_scalar(g.w_exact[0:1, :], p_flag[0:1, 0:1], 0.0, None, ALU.is_le)
        dve.wait_ge(std_ready, 2)
        ln_apply(nc, g, step, 1, x2, lambda j: g.xf[:, j])
        assert step.n == MIX_STEPS
        for b in range(2):
            dve.wait_ge(xt_ready, b + 1)
            split_xf(nc, dve, g, b, banks[b], split, 2 * b)

    parts = Shared()
    parts.sync, parts.tensor, parts.gpsimd, parts.scalar, parts.vector = sync, tensor, gpsimd, scalar, vector
    return parts


def ffn(nc, g, s_, wffn, x, attn_t, out):
    passed, S, S3, xfT, xs, x2 = g.passed, g.S, g.S3, g.xfT, g.xs, g.x2
    with ExitStack() as ctx:
        def sem(name):
            return ctx.enter_context(nc.semaphore(name))

        gate = [s_(f"gate{i}", [P, QW]) for i in range(2)]
        y = s_("y", [P, TG, D])
        ob = s_("ob", [P, TG, D])
        N_TEMP = 3
        temp = [s_(f"temp{i}", [P, QW]) for i in range(N_TEMP)]
        whole = Arena(nc, s_.at)
        ha = whole("ha", [P, HC, QW])
        hb = whole("hb", [P, HC, QW])
        ha_s = s_("ha_s", [P, 2, HC, QW], F32R)
        hb_s = s_("hb_s", [P, 2, HC, QW], F32R)
        NBK = 6
        USES = 2 * HC + HC + HC + TG
        CHUNKS = 3 * HC
        assert USES % NBK == 0 and CHUNKS % N_TEMP == 0
        bank = [ctx.enter_context(nc.psum_tensor(f"bank{i}", [P, QW], F32)) for i in range(NBK)]
        p_mix = [ctx.enter_context(nc.psum_tensor(f"p_mix{i}", [P, QW], F32)) for i in range(2)]
        w_in = sem("w_in")
        at_in = sem("at_in_f")
        x_in = sem("x_in_f")
        pe_ready = sem("pe_ready")
        gate_ready = sem("gate_ready")
        h1_ready = sem("h1_ready")
        h23_ready = sem("h23_ready")
        xs_ready = sem("xs_ready")
        parts_ready = sem("parts_ready")
        y_ready = sem("y3_ready")
        step_f = sem("step_f")
        step_m = sem("step_mf")
        var_f = sem("var_f")
        std_f = sem("std_f")
        var_m = sem("var_mf")
        std_m = sem("std_mf")
        y_made = sem("y_made_f")
        xt_ready = sem("xt_f")
        ob_ready = sem("ob_ready")
        out_done = sem("out_done")
        LN_STEPS = 2 * TG + 1 + TG
        NPARTS = 2 * CHUNKS
        ov = out.rearrange("(g t p) d -> g p t d", t=TG, p=P)

        def weights(Wx):
            flat = Wx[:].rearrange("p q e -> p (q e)")
            cut, mats = 0, []
            for rows, cols in ((D, HID), (D, HID), (HID, D), (HID, HID), (HID, HID)):
                size = rows // P * cols
                mats.append(flat[:, cut:cut + size].rearrange("p (c n) -> p c n", n=cols))
                cut += size
            return mats

        def by_weights(eng, program):
            exact = eng.value_load(g.w_exact[0:1, 0:1], min_val=0, max_val=1)
            with eng.If(exact == 1):
                program(True)
            with eng.If(exact == 0):
                program(False)

        with nc.Block() as block:
            @block.sync
            def _(sp):
                sp.nop().then_inc(out_done, 16)
                load_at(sp, g, attn_t, 1, at_in)
                load_x(sp, g, x, 1, x_in)
                with sp.If(sp.value_load(g.w_exact[0:1, 0:1], min_val=0, max_val=1) == 0):
                    for i in range(W_CHUNKS):
                        sp.dma_start(g.Wf[:, i, :], wffn[i]).then_inc(w_in, 16)
                    sp.wait_ge(w_in, W_CHUNKS * 16)

                def store(turn):
                    sp.dma_start(ov[turn], ob[:]).then_inc(out_done, 16)

                def body(it, first, last):
                    if not last:
                        wait_apart(sp, passed, y_made, at(it, TG, TG))
                        load_at(sp, g, attn_t, (it + 2) % NG, at_in)
                    if not first:
                        wait_apart(sp, passed, ob_ready, it)
                        store(it - 1)
                    if not last:
                        wait_apart(sp, passed, step_m, at(it, MIX_STEPS, MIX_X2))
                        load_x(sp, g, x, (it + 2) % NG, x_in)
                peeled(sp, NG, body)
                sp.wait_ge(ob_ready, NG)
                store(NG - 1)
                sp.wait_ge(out_done, (NG + 1) * 16)
                sp.wait_ge(at_in, NG * 16)
                sp.wait_ge(x_in, NG * 16)

            @block.tensor
            def _(pe):
                def wait_read(it, n):
                    turn, n = (0, n) if n >= 0 else (-1, n + USES)
                    if n >= 4 * HC:
                        pe.wait_ge(y_ready, at(it, TG, TG + TG * turn + n - 4 * HC + 1))
                    elif n >= 2 * HC:
                        pe.wait_ge(h23_ready, at(it, 2 * HC, 2 * HC + 2 * HC * turn + n - 2 * HC + 1))
                    elif n % 2:
                        pe.wait_ge(h1_ready, at(it, HC, 2 + n // 2 + 1))
                    else:
                        pe.wait_ge(gate_ready, at(it, HC, n // 2 + 1))

                def program(exact):
                    W1, W2, W3, H1, H2 = weights(g.Wr if exact else g.Wf)
                    order = [(p, c) for p in range(2) for c in range(HC - 1)] + [(0, HC - 1), (1, HC - 1)]
                    if not exact:
                        pe.wait_ge(w_in, W_CHUNKS * 16)

                    def body(it, first, last):
                        n = 0

                        def use(width, steps, *more):
                            nonlocal n
                            products = (steps,) + more
                            cuts = [range(len(steps) - 2), range(len(steps) - 2, len(steps))] if more else [range(len(steps))]
                            for ks in cuts:
                                for u, product in enumerate(products):
                                    if ks.start == 0:
                                        wait_read(it, n + u - NBK)
                                    for k in ks:
                                        w, m, part = product[k]
                                        if part is not None:
                                            pe.wait_ge(parts_ready, at(it, NPARTS, 2 * N_TEMP + part + 1))
                                        ins = pe.matmul(bank[(n + u) % NBK][:, 0:width], w, m, start=(k == 0),
                                                        stop=(k == len(product) - 1))
                                    if ks.stop == len(product):
                                        ins.then_inc(pe_ready, 1)
                            n += len(products)

                        pe.wait_ge(xs_ready, at(it, 2 * DC, 2 * DC))
                        for m in range(HC):
                            for W in (W1, W2):
                                col = slice(m * P, (m + 1) * P)
                                if exact:
                                    use(QW, [(W[:, c, col], xs[:, p, c, :], None) for p in range(2) for c in range(DC)])
                                else:
                                    use(QW, [(W[:, c, col], xfT[:, c, :], None) for c in range(DC)])
                        if not last:
                            pe.wait_ge(at_in, at(it, 16, 16))
                            project(pe, g, p_mix, y_made)
                        for layer, (W, src_s, src) in enumerate(((H1, ha_s, ha), (H2, hb_s, hb))):
                            if layer == 1 and not last:
                                wait_apart(pe, passed, step_m, at(it, MIX_STEPS, MIX_STEPS))
                                turn_xf(pe, g, p_mix, xt_ready)
                            if not exact:
                                pe.wait_ge(*((h1_ready, at(it, HC, HC + 2)),
                                             (h23_ready, at(it, 2 * HC, 3 * HC)))[layer])
                            for m in range(HC):
                                col = slice(m * P, (m + 1) * P)
                                if exact:
                                    use(QW, [(W[:, c, col], src_s[:, p, c, :],
                                              2 * (layer * HC + c) + p if m == 0 else None) for p, c in order])
                                else:
                                    use(QW, [(W[:, c, col], src[:, c, :], None) for c in range(HC)])
                        if not exact:
                            pe.wait_ge(h23_ready, at(it, 2 * HC, 4 * HC))
                        toks = [slice(j * P, (j + 1) * P) for j in range(TG)]
                        if exact:
                            use(D, *[[(ha_s[:, p, c, toks[j]], W3[:, c, :], 2 * (2 * HC + c) + p if j == 0 else None)
                                      for p, c in order] for j in range(TG)])
                        else:
                            for tok in toks:
                                use(D, [(ha[:, c, tok], W3[:, c, :], None) for c in range(HC)])
                    peeled(pe, NG, body)
                by_weights(pe, program)

            @block.scalar
            def _(act):
                act.nop().then_inc(h23_ready, 2 * HC)

                def tail(turn):
                    act.wait_ge(var_f, turn + 1)
                    nc.scalar.activation(g.sd[:, 2], g.mv[:, 2, :, 1], ACT.Sqrt).then_inc(std_f, 1)

                def program(exact):
                    def body(it, first, last):
                        for m in range(HC):
                            n = 2 * m
                            act.wait_ge(pe_ready, at(it, USES, n + 1))
                            act.wait_ge(h1_ready, at(it, HC, m + 1))
                            nc.scalar.activation(gate[m % 2][:], bank[n % NBK][:], ACT.Silu,
                                                 scale=S[:, 0, m:m + 1]).then_inc(gate_ready, 1)
                        if not first:
                            tail(it - 1)
                        if not last:
                            for k in range(2):
                                act.wait_ge(var_m, at(it, 2, k + 1))
                                nc.scalar.activation(g.sd[:, k], g.mv[:, k, :, 1], ACT.Sqrt).then_inc(std_m, 1)
                        for layer, whole_out in ((2, hb), (3, ha)):
                            for m in range(HC):
                                n = layer * HC + m
                                k = (layer - 1) * HC + m
                                act.wait_ge(pe_ready, at(it, USES, n + 1))
                                if exact:
                                    act.wait_ge(parts_ready, at(it, NPARTS, 2 * k + 2))
                                dst = temp[k % N_TEMP][:] if exact else whole_out[:, m, :]
                                nc.scalar.activation(dst, bank[n % NBK][:], ACT.Gelu,
                                                     scale=S[:, layer, m:m + 1]).then_inc(h23_ready, 1)
                    peeled(act, NG, body)
                    tail(NG - 1)
                by_weights(act, program)

            @block.vector
            def _(dve):
                dve.nop().then_inc(h1_ready, 2)
                dve.nop().then_inc(y_ready, TG)
                dve.nop().then_inc(parts_ready, 2 * N_TEMP)

                def split(it, k, dst, m):
                    t = temp[k % N_TEMP]
                    nc.vector.tensor_copy(dst[:, 0, m], t[:]).then_inc(parts_ready, 1)
                    dve.wait_ge(parts_ready, at(it, NPARTS, 2 * N_TEMP + 2 * k + 1))
                    nc.vector.tensor_tensor(dst[:, 1, m], t[:], dst[:, 0, m].bitcast(F32),
                                            ALU.subtract).then_inc(parts_ready, 1)

                def y_tile(j):
                    return y[:, j]

                def mix_y(j):
                    return p_mix[j // 2][:, (j % 2) * D:(j % 2 + 1) * D]

                def tail_end(turn, step):
                    dve.wait_ge(std_f, turn + 1)
                    ln_apply(nc, g, step, 2, y_tile, y_tile)
                    step.join()
                    assert step.n == LN_STEPS
                    dve.wait_ge(out_done, at(turn, 16, 16))
                    nc.vector.tensor_tensor(ob[:], y[:], x2[:, turn % 2], ALU.add).then_inc(ob_ready, 1)
                    wait_apart(dve, passed, ob_ready, turn + 1)

                def tail_start(turn):
                    step = Chain(dve, passed, step_f, at(turn, LN_STEPS, 0))
                    wait_apart(dve, passed, y_ready, at(turn, TG, 2 * TG))
                    ln_stats(nc, g, step, 2, y_tile, var_f)
                    return step

                def program(exact):
                    if exact:
                        dve.nop().then_inc(xs_ready, 2 * DC)
                    else:
                        nc.vector.tensor_tensor(xfT[:], xs[:, 0].bitcast(F32), xs[:, 1].bitcast(F32),
                                                ALU.add).then_inc(xs_ready, 2 * DC)

                    def body(it, first, last):
                        for m in range(HC):
                            n = 2 * m + 1
                            dve.wait_ge(pe_ready, at(it, USES, n + 1))
                            dve.wait_ge(gate_ready, at(it, HC, m + 1))
                            if exact:
                                dve.wait_ge(parts_ready, at(it, NPARTS, 2 * m + 2))
                            dst = temp[m % N_TEMP][:] if exact else ha[:, m, :]
                            nc.vector.scalar_tensor_tensor(out=dst, in0=bank[n % NBK][:], scalar=S[:, 1, m:m + 1],
                                                           in1=gate[m % 2][:], op0=ALU.mult,
                                                           op1=ALU.mult).then_inc(h1_ready, 1)
                            if exact:
                                dve.wait_ge(h1_ready, at(it, HC, 2 + m + 1))
                                split(it, m, ha_s, m)
                        if not first:
                            step_t = tail_start(it - 1)
                        if not last:
                            slot = (it + 1) % 2
                            step = Chain(dve, passed, step_m, at(it, MIX_STEPS, 0))
                            wait_apart(dve, passed, y_made, at(it, TG, TG))
                            ln_stats(nc, g, step, 0, mix_y, var_m)
                        if not first:
                            tail_end(it - 1, step_t)
                        if not last:
                            dve.wait_ge(std_m, at(it, 2, 1))
                            ln_apply(nc, g, step, 0, mix_y, lambda j: x2[:, slot, j])
                            step.join()
                            dve.wait_ge(x_in, at(it, 16, 16))
                            step(nc.vector.tensor_tensor(x2[:, slot], x2[:, slot], g.x_in[:], ALU.add))
                            assert step.n == MIX_X2
                            ln_stats(nc, g, step, 1, lambda j: x2[:, slot, j], var_m)
                            dve.wait_ge(std_m, at(it, 2, 2))
                            ln_apply(nc, g, step, 1, lambda j: x2[:, slot, j], lambda j: g.xf[:, j])
                            assert step.n == MIX_STEPS
                        for layer, dst in ((2, hb_s), (3, ha_s)):
                            if exact:
                                for m in range(HC):
                                    dve.wait_ge(h23_ready, at(it, 2 * HC, 2 * HC + (layer - 2) * HC + m + 1))
                                    split(it, (layer - 1) * HC + m, dst, m)
                            if layer == 2 and not last:
                                for b in range(2):
                                    dve.wait_ge(xt_ready, at(it, 2, b + 1))
                                    if exact:
                                        split_xf(nc, dve, g, b, p_mix[b][:], xs_ready, at(it, 2 * DC, 2 * DC + 2 * b))
                                    else:
                                        nc.vector.tensor_copy(by_token(xfT[:], b),
                                                              bank_tokens(p_mix[b][:])).then_inc(xs_ready, 2)
                        for j in range(TG):
                            n = 4 * HC + j
                            dve.wait_ge(pe_ready, at(it, USES, n + 1))
                            nc.vector.tensor_tensor(y[:, j], bank[n % NBK][:, 0:D], S3[:], ALU.mult).then_inc(y_ready, 1)
                    peeled(dve, NG, body)
                    tail_end(NG - 1, tail_start(NG - 1))
                by_weights(dve, program)


def kernel(L0_attn_x, L0_attn_Wq, L0_attn_Wk, L0_attn_Wv, L0_attn_Wo, L0_attn_q_norm_w, L0_attn_k_norm_w,
           L0_ffn_w1_w, L0_ffn_w1_s, L0_ffn_w2_w, L0_ffn_w2_s, L0_ffn_h1_w, L0_ffn_h1_s, L0_ffn_h2_w,
           L0_ffn_h2_s, L0_ffn_w3_w, L0_ffn_w3_s):
    import concourse.bacc as bacc
    from concourse.bass_utils import run_bass_kernel_spmd

    def chunks(w):
        w = np.asarray(w).T
        w = w.reshape(-1, P, w.shape[1]).transpose(1, 0, 2).reshape(P, -1, W_CHUNK)
        return w.transpose(1, 0, 2)

    def columns(s):
        return np.ascontiguousarray(np.asarray(s).reshape(HC, P).T)

    inv_freq = (1.0 / np.float32(10000.0) ** (np.arange(0, HD, 2, dtype=np.float32) / np.float32(HD)))
    angle = np.outer(np.arange(T, dtype=np.float32), inv_freq.astype(np.float32)).astype(np.float32)
    arrays = {
        "x": np.ascontiguousarray(np.asarray(L0_attn_x).reshape(B * T, D)),
        "wq": np.asarray(L0_attn_Wq), "wk": np.asarray(L0_attn_Wk), "wv": np.asarray(L0_attn_Wv),
        "wo": np.asarray(L0_attn_Wo), "qw": np.asarray(L0_attn_q_norm_w), "kw": np.asarray(L0_attn_k_norm_w),
        "cos": np.cos(angle), "sin": np.sin(angle),
        "wffn": np.ascontiguousarray(np.concatenate(
            [chunks(w) for w in (L0_ffn_w1_w, L0_ffn_w2_w, L0_ffn_w3_w, L0_ffn_h1_w, L0_ffn_h2_w)])),
        "w1s": columns(L0_ffn_w1_s), "w2s": columns(L0_ffn_w2_s),
        "h1s": columns(L0_ffn_h1_s), "h2s": columns(L0_ffn_h2_s), "w3s": np.asarray(L0_ffn_w3_s),
    }
    nc = bacc.Bacc("TRN2", target_bir_lowering=False, num_devices=1)
    args = [nc.dram_tensor(n, a.shape, mybir.dt.from_np(a.dtype), kind="ExternalInput").ap()
            for n, a in arrays.items()]
    out = nc.dram_tensor("out", (B * T, D), F32, kind="ExternalOutput").ap()
    build(nc, *args, out)
    r = run_bass_kernel_spmd(nc, [arrays], core_ids=[0])
    return r.results[0]["out"].reshape(B, T, D)
```
